# Optimizing a Trainium2 kernel written in Bass

```python
import numpy as np
import jax
import jax.numpy as jnp

def _softmax(x, axis=-1):
    return jax.nn.softmax(x, axis=axis)
def _gelu(x):
    return jax.nn.gelu(x, approximate=True)
def _silu(x):
    return jax.nn.silu(x)
def _sigmoid(x):
    return jax.nn.sigmoid(x)
def _layernorm(x, axis=-1, eps=1e-5):
    m = jnp.mean(x, axis=axis, keepdims=True)
    v = jnp.var(x, axis=axis, keepdims=True)
    return (x - m) / jnp.sqrt(v + eps)
def _scatter_add(tgt, idx, src, axis=0):
    return tgt.at[idx].add(src)
def _segment_sum(src, seg, n):
    return jax.ops.segment_sum(src, seg, n)

kernel_name = 'mk_conv_preact_d2_conv_nchw192_226302'

def setup_inputs(seed: int = 0):
    np.random.seed(seed)
    _w = jnp.asarray
    def _rec_inputs():
        import jax
        import jax.numpy as jnp
        _gk = jax.random.key(seed)
        x = -4.65e-05 + 0.9999 * jax.random.normal(jax.random.fold_in(_gk, 1), (16, 192, 128, 128), jnp.float32)
        return x
    x = _rec_inputs()
    def _L0_conv_setup():
        import jax, jax.numpy as jnp
        import numpy as np
        from jax import lax
        key = jax.random.key(seed)
        k1, k2, k3 = jax.random.split(key, 3)
        B, C, H, W = (16, 192, 128, 128)
        x = jax.random.normal(k1, (B, C, H, W), dtype=jnp.float32)
        fan_in = 9.0
        bound = 1.0 / np.sqrt(fan_in)
        w = jax.random.uniform(k2, (1, 1, 3, 3), jnp.float32, -bound, bound)
        b = jax.random.uniform(k3, (1,), jnp.float32, -bound, bound)
        return {'x': x, 'w': w, 'b': b}
    _L0_conv_all = _L0_conv_setup()
    _L0_conv_in = {k: v for k, v in _L0_conv_all.items() if k in ('w', 'b', )}
    del _L0_conv_all

    def _L1_conv_setup():
        import jax, jax.numpy as jnp
        import numpy as np
        import math
        C64 = jnp.complex64

        def _fftconv_full(a, kern):
            L = a.shape[-1] + kern.shape[0] - 1
            A = jnp.fft.fft(a, n=L, axis=-1)
            K = jnp.fft.fft(kern.astype(a.dtype), n=L)
            return jnp.fft.ifft(A * K, axis=-1)

        def _centered_ifft(f):
            N = f.shape[-1]
            shft = (np.arange(N) + int(np.fix(N / 2))) % N
            inv = np.argsort(shft)
            g = jnp.fft.ifft(f[..., shft], axis=-1) * math.sqrt(N)
            return g[..., inv].astype(f.dtype)

        def _sincinterp(f):
            N = f.shape[-1]
            y = jnp.zeros(f.shape[:-1] + (2 * N - 1,), f.dtype).at[..., ::2].set(f)
            kern = jnp.asarray(np.sinc(np.arange(-(2 * N - 3), 2 * N - 2) / 2.0).astype(np.complex64))
            return _fftconv_full(y, kern)[..., 2 * N - 3:4 * N - 4]

        def _frft_chirp(f, a):
            N = f.shape[-1]
            alpha = a * math.pi / 2
            tana2, sina = (math.tan(alpha / 2), math.sin(alpha))
            fi = _sincinterp(f)
            pad = jnp.zeros(f.shape[:-1] + (N - 1,), f.dtype)
            fp = jnp.concatenate([pad, fi, pad], axis=-1)
            n = np.arange(-2 * N + 2, 2 * N - 1).astype(np.float64)
            chrp = jnp.asarray(np.exp(-1j * math.pi / N * tana2 / 4 * n ** 2).astype(np.complex64))
            fp = chrp * fp
            c = math.pi / N / sina / 4
            m = np.arange(-(4 * N - 4), 4 * N - 3).astype(np.float64)
            kern = jnp.asarray(np.exp(1j * c * m ** 2).astype(np.complex64))
            ret = _fftconv_full(fp, kern)[..., 4 * N - 4:8 * N - 7] * math.sqrt(c / math.pi)
            ret = chrp * ret
            phase = np.complex64(np.exp(-1j * (1 - a) * math.pi / 4))
            return phase * ret[..., N - 1:3 * N - 2:2]

        def _frft_last(f, a):
            if a < 0.5:
                f = _centered_ifft(f)
                a = a + 1.0
            return _frft_chirp(f, a)

        def _frft2d(x, a):
            t = _frft_last(x, a)
            return jnp.swapaxes(_frft_last(jnp.swapaxes(t, -1, -2), a), -1, -2)

        def _c1x1(x, w, b=None):
            y = jnp.einsum('nchw,oc->nohw', x, w)
            return y if b is None else y + b[None, :, None, None]

        def _c3x3(x, w, b):
            y = jax.lax.conv_general_dilated(x, w, (1, 1), 'SAME', dimension_numbers=('NCHW', 'OIHW', 'NCHW'))
            return y + b[None, :, None, None]

        def _forward(x, conv1_w, mag_s_w, mag_s_b, mag_f_w, mag_f_b, mag_w, mag_b, pha_w, pha_b, conv_0_w, conv_0_b, conv_1_w, conv_1_b, conv2_w):
            angle = 0.5
            alpha = math.cos(angle * math.pi / 2)
            N, C, H, W = x.shape
            H1, W1 = (int(H * alpha), int(W * alpha))
            x1 = _c1x1(x, conv1_w)
            C1, C0 = (C // 4, C // 4 // 3)
            x_0, x_05, x_1 = (x1[:, :C0], x1[:, C0:C1 - C0], x1[:, C1 - C0:C1])
            h0, w0 = ((H - H1) // 2, (W - W1) // 2)
            mask1 = jnp.zeros((H, W), jnp.float32).at[h0:h0 + H1, w0:w0 + W1].set(1.0)
            mask2 = 1.0 - mask1
            Fre = _frft2d(x_05.astype(C64), angle)
            mag, pha = (jnp.abs(Fre), jnp.angle(Fre))
            mag_out = _c1x1(_c3x3(mag * mask1, mag_s_w, mag_s_b) * mask1 + _c1x1(mag * mask2, mag_f_w, mag_f_b) * mask2, mag_w, mag_b)
            pha_out = _c1x1(pha, pha_w, pha_b)
            Fre_out = jax.lax.complex(mag_out * jnp.cos(pha_out), mag_out * jnp.sin(pha_out))
            ifrft = jnp.abs(_frft2d(Fre_out, -angle))
            fre = jnp.fft.rfft2(x_1)
            fm, fp = (jnp.abs(fre), jnp.angle(fre))
            mo = _c1x1(fm, conv_1_w, conv_1_b)
            po = _c1x1(fp, conv_1_w, conv_1_b)
            x_1o = jnp.fft.irfft2(jax.lax.complex(mo * jnp.cos(po), mo * jnp.sin(po)), s=(H, W))
            x_0o = _c1x1(x_0, conv_0_w, conv_0_b)
            return _c1x1(jnp.concatenate([x_0o, ifrft, x_1o], axis=1), conv2_w)
        key = jax.random.key(seed)
        ks = jax.random.split(key, 16)
        N, C, H, W, Co = (4, 192, 128, 128, 192)
        C1, C0 = (C // 4, C // 4 // 3)
        Cm = C1 - 2 * C0
        s = 0.05
        r = lambda k, sh: jax.random.normal(k, sh, jnp.float32)
        return {'x': r(ks[0], (N, C, H, W)), 'conv1_w': r(ks[1], (C1, C)) * s, 'mag_s_w': r(ks[2], (Cm, Cm, 3, 3)) * s, 'mag_s_b': r(ks[3], (Cm,)) * s, 'mag_f_w': r(ks[4], (Cm, Cm)) * s, 'mag_f_b': r(ks[5], (Cm,)) * s, 'mag_w': r(ks[6], (Cm, Cm)) * s, 'mag_b': r(ks[7], (Cm,)) * s, 'pha_w': r(ks[8], (Cm, Cm)) * s, 'pha_b': r(ks[9], (Cm,)) * s, 'conv_0_w': r(ks[10], (C0, C0)) * s, 'conv_0_b': r(ks[11], (C0,)) * s, 'conv_1_w': r(ks[12], (C0, C0)) * s, 'conv_1_b': r(ks[13], (C0,)) * s, 'conv2_w': r(ks[14], (Co, C1)) * s}
    _L1_conv_all = _L1_conv_setup()
    _L1_conv_in = {k: v for k, v in _L1_conv_all.items() if k in ('conv1_w', 'mag_s_w', 'mag_s_b', 'mag_f_w', 'mag_f_b', 'mag_w', 'mag_b', 'pha_w', 'pha_b', 'conv_0_w', 'conv_0_b', 'conv_1_w', 'conv_1_b', 'conv2_w', )}
    del _L1_conv_all

    return {
        "x": x,
        "L0_conv_w": _L0_conv_in["w"],
        "L0_conv_b": _L0_conv_in["b"],
        "L1_conv_conv1_w": _L1_conv_in["conv1_w"],
        "L1_conv_mag_s_w": _L1_conv_in["mag_s_w"],
        "L1_conv_mag_s_b": _L1_conv_in["mag_s_b"],
        "L1_conv_mag_f_w": _L1_conv_in["mag_f_w"],
        "L1_conv_mag_f_b": _L1_conv_in["mag_f_b"],
        "L1_conv_mag_w": _L1_conv_in["mag_w"],
        "L1_conv_mag_b": _L1_conv_in["mag_b"],
        "L1_conv_pha_w": _L1_conv_in["pha_w"],
        "L1_conv_pha_b": _L1_conv_in["pha_b"],
        "L1_conv_conv_0_w": _L1_conv_in["conv_0_w"],
        "L1_conv_conv_0_b": _L1_conv_in["conv_0_b"],
        "L1_conv_conv_1_w": _L1_conv_in["conv_1_w"],
        "L1_conv_conv_1_b": _L1_conv_in["conv_1_b"],
        "L1_conv_conv2_w": _L1_conv_in["conv2_w"],
    }

def reference(x, L0_conv_w, L0_conv_b, L1_conv_conv1_w, L1_conv_mag_s_w, L1_conv_mag_s_b, L1_conv_mag_f_w, L1_conv_mag_f_b, L1_conv_mag_w, L1_conv_mag_b, L1_conv_pha_w, L1_conv_pha_b, L1_conv_conv_0_w, L1_conv_conv_0_b, L1_conv_conv_1_w, L1_conv_conv_1_b, L1_conv_conv2_w):
    import jax
    import jax.numpy as jnp
    def _L0_conv_ref(x, w, b):
        import jax, jax.numpy as jnp
        import numpy as np
        from jax import lax
        B, C, H, W = x.shape
        xr = x.reshape(B * C, 1, H, W)
        y = lax.conv_general_dilated(xr, w, window_strides=(1, 1), padding=((1, 1), (1, 1)), dimension_numbers=('NCHW', 'OIHW', 'NCHW'))
        y = y + b[None, :, None, None]
        return y.reshape(B, C, H, W)

    def _L1_conv_ref(x, conv1_w, mag_s_w, mag_s_b, mag_f_w, mag_f_b, mag_w, mag_b, pha_w, pha_b, conv_0_w, conv_0_b, conv_1_w, conv_1_b, conv2_w):
        import jax, jax.numpy as jnp
        import numpy as np
        import math
        C64 = jnp.complex64

        def _fftconv_full(a, kern):
            L = a.shape[-1] + kern.shape[0] - 1
            A = jnp.fft.fft(a, n=L, axis=-1)
            K = jnp.fft.fft(kern.astype(a.dtype), n=L)
            return jnp.fft.ifft(A * K, axis=-1)

        def _centered_ifft(f):
            N = f.shape[-1]
            shft = (np.arange(N) + int(np.fix(N / 2))) % N
            inv = np.argsort(shft)
            g = jnp.fft.ifft(f[..., shft], axis=-1) * math.sqrt(N)
            return g[..., inv].astype(f.dtype)

        def _sincinterp(f):
            N = f.shape[-1]
            y = jnp.zeros(f.shape[:-1] + (2 * N - 1,), f.dtype).at[..., ::2].set(f)
            kern = jnp.asarray(np.sinc(np.arange(-(2 * N - 3), 2 * N - 2) / 2.0).astype(np.complex64))
            return _fftconv_full(y, kern)[..., 2 * N - 3:4 * N - 4]

        def _frft_chirp(f, a):
            N = f.shape[-1]
            alpha = a * math.pi / 2
            tana2, sina = (math.tan(alpha / 2), math.sin(alpha))
            fi = _sincinterp(f)
            pad = jnp.zeros(f.shape[:-1] + (N - 1,), f.dtype)
            fp = jnp.concatenate([pad, fi, pad], axis=-1)
            n = np.arange(-2 * N + 2, 2 * N - 1).astype(np.float64)
            chrp = jnp.asarray(np.exp(-1j * math.pi / N * tana2 / 4 * n ** 2).astype(np.complex64))
            fp = chrp * fp
            c = math.pi / N / sina / 4
            m = np.arange(-(4 * N - 4), 4 * N - 3).astype(np.float64)
            kern = jnp.asarray(np.exp(1j * c * m ** 2).astype(np.complex64))
            ret = _fftconv_full(fp, kern)[..., 4 * N - 4:8 * N - 7] * math.sqrt(c / math.pi)
            ret = chrp * ret
            phase = np.complex64(np.exp(-1j * (1 - a) * math.pi / 4))
            return phase * ret[..., N - 1:3 * N - 2:2]

        def _frft_last(f, a):
            if a < 0.5:
                f = _centered_ifft(f)
                a = a + 1.0
            return _frft_chirp(f, a)

        def _frft2d(x, a):
            t = _frft_last(x, a)
            return jnp.swapaxes(_frft_last(jnp.swapaxes(t, -1, -2), a), -1, -2)

        def _c1x1(x, w, b=None):
            y = jnp.einsum('nchw,oc->nohw', x, w)
            return y if b is None else y + b[None, :, None, None]

        def _c3x3(x, w, b):
            y = jax.lax.conv_general_dilated(x, w, (1, 1), 'SAME', dimension_numbers=('NCHW', 'OIHW', 'NCHW'))
            return y + b[None, :, None, None]

        def _forward(x, conv1_w, mag_s_w, mag_s_b, mag_f_w, mag_f_b, mag_w, mag_b, pha_w, pha_b, conv_0_w, conv_0_b, conv_1_w, conv_1_b, conv2_w):
            angle = 0.5
            alpha = math.cos(angle * math.pi / 2)
            N, C, H, W = x.shape
            H1, W1 = (int(H * alpha), int(W * alpha))
            x1 = _c1x1(x, conv1_w)
            C1, C0 = (C // 4, C // 4 // 3)
            x_0, x_05, x_1 = (x1[:, :C0], x1[:, C0:C1 - C0], x1[:, C1 - C0:C1])
            h0, w0 = ((H - H1) // 2, (W - W1) // 2)
            mask1 = jnp.zeros((H, W), jnp.float32).at[h0:h0 + H1, w0:w0 + W1].set(1.0)
            mask2 = 1.0 - mask1
            Fre = _frft2d(x_05.astype(C64), angle)
            mag, pha = (jnp.abs(Fre), jnp.angle(Fre))
            mag_out = _c1x1(_c3x3(mag * mask1, mag_s_w, mag_s_b) * mask1 + _c1x1(mag * mask2, mag_f_w, mag_f_b) * mask2, mag_w, mag_b)
            pha_out = _c1x1(pha, pha_w, pha_b)
            Fre_out = jax.lax.complex(mag_out * jnp.cos(pha_out), mag_out * jnp.sin(pha_out))
            ifrft = jnp.abs(_frft2d(Fre_out, -angle))
            fre = jnp.fft.rfft2(x_1)
            fm, fp = (jnp.abs(fre), jnp.angle(fre))
            mo = _c1x1(fm, conv_1_w, conv_1_b)
            po = _c1x1(fp, conv_1_w, conv_1_b)
            x_1o = jnp.fft.irfft2(jax.lax.complex(mo * jnp.cos(po), mo * jnp.sin(po)), s=(H, W))
            x_0o = _c1x1(x_0, conv_0_w, conv_0_b)
            return _c1x1(jnp.concatenate([x_0o, ifrft, x_1o], axis=1), conv2_w)
        return _forward(x, conv1_w, mag_s_w, mag_s_b, mag_f_w, mag_f_b, mag_w, mag_b, pha_w, pha_b, conv_0_w, conv_0_b, conv_1_w, conv_1_b, conv2_w)

    def _gn(v, G=32, eps=1e-5):
        B_, C_, H_, W_ = v.shape
        g = v.reshape(B_, G, C_ // G, H_, W_)
        m = jnp.mean(g, axis=(2, 3, 4), keepdims=True)
        s = jnp.var(g, axis=(2, 3, 4), keepdims=True)
        return ((g - m) / jnp.sqrt(s + eps)).reshape(v.shape)

    def _ln_c(v, eps=1e-6):
        m = jnp.mean(v, axis=1, keepdims=True)
        s = jnp.var(v, axis=1, keepdims=True)
        return (v - m) / jnp.sqrt(s + eps)

    def _ln_t(v, eps=1e-5):
        m = jnp.mean(v, axis=-1, keepdims=True)
        s = jnp.var(v, axis=-1, keepdims=True)
        return (v - m) / jnp.sqrt(s + eps)

    def _to_tokens(v):
        B_, C_, H_, W_ = v.shape
        return v.reshape(B_, C_, H_ * W_).transpose(0, 2, 1)
    def _from_tokens(t, like):
        B_, C_, H_, W_ = like.shape
        return t.transpose(0, 2, 1).reshape(B_, C_, H_, W_)

    x = x + _L0_conv_ref(_gn(x), L0_conv_w, L0_conv_b)
    x = x + _L1_conv_ref(_gn(x), L1_conv_conv1_w, L1_conv_mag_s_w, L1_conv_mag_s_b, L1_conv_mag_f_w, L1_conv_mag_f_b, L1_conv_mag_w, L1_conv_mag_b, L1_conv_pha_w, L1_conv_pha_b, L1_conv_conv_0_w, L1_conv_conv_0_b, L1_conv_conv_1_w, L1_conv_conv_1_b, L1_conv_conv2_w)
    return x


_drawn_inputs = setup_inputs


def setup_inputs(seed=0):
    import zlib

    import numpy as np

    out = dict(_drawn_inputs(seed))
    spreads = {}
    factors = {'L1_conv_mag_s_w': 7.838,
     'L1_conv_mag_s_b': 8.0,
     'L1_conv_mag_f_w': 8.0,
     'L1_conv_mag_f_b': 8.0,
     'L1_conv_mag_w': 8.0,
     'L1_conv_mag_b': 8.0,
     'L1_conv_pha_w': 8.0,
     'L1_conv_pha_b': 64.0,
     'L1_conv_conv_0_b': 4.945,
     'L1_conv_conv_1_b': 64.0,
     'L1_conv_conv_1_w': 2.871}
    for name, (base, spread) in spreads.items():
        noise = np.random.default_rng([zlib.crc32(name.encode()), seed]).standard_normal(out[name].shape)
        drawn = base * np.exp(spread * noise) if base else spread * noise
        out[name] = jnp.asarray(drawn.astype(out[name].dtype))
    for name, factor in factors.items():
        out[name] = (out[name] * factor).astype(out[name].dtype)
    return out
```

```python
import math
from contextlib import ExitStack

import numpy as np
import concourse.bass as bass
from concourse import mybir

N, C, H, W = 16, 192, 128, 128
G, CG = 32, 6
Q = 4
LOADS = 4
GQ, CQ = G // Q, C // Q
C1, C0 = C // 4, C // 12
HALF = C // 2
KW = W // 2 + 1
LO = (H - int(H * math.cos(math.pi / 4))) // 2
BOX = int(H * math.cos(math.pi / 4))
WB = 8
WO = WB - 2
NBOX = BOX // WO
T = 2 * (C1 + 1)
EPS = 1e-5
ROUND = 12582912.0
TWO_PI = 6.283185
assert BOX % WO == 0


def frft_matrices():
    n_ = W

    def fftconv(a, kern):
        length = a.shape[-1] + kern.shape[0] - 1
        return np.fft.ifft(np.fft.fft(a, n=length, axis=-1) * np.fft.fft(kern, n=length), axis=-1)

    def chirp(f, a):
        alpha = a * math.pi / 2
        tana2, sina = math.tan(alpha / 2), math.sin(alpha)
        y = np.zeros(f.shape[:-1] + (2 * n_ - 1,), np.complex128)
        y[..., ::2] = f
        fi = fftconv(y, np.sinc(np.arange(-(2 * n_ - 3), 2 * n_ - 2) / 2.0))[..., 2 * n_ - 3:4 * n_ - 4]
        pad = np.zeros(f.shape[:-1] + (n_ - 1,), np.complex128)
        n = np.arange(-2 * n_ + 2, 2 * n_ - 1).astype(np.float64)
        chrp = np.exp(-1j * math.pi / n_ * tana2 / 4 * n ** 2)
        c = math.pi / n_ / sina / 4
        m = np.arange(-(4 * n_ - 4), 4 * n_ - 3).astype(np.float64)
        ret = fftconv(chrp * np.concatenate([pad, fi, pad], axis=-1), np.exp(1j * c * m ** 2))
        ret = chrp * (ret[..., 4 * n_ - 4:8 * n_ - 7] * math.sqrt(c / math.pi))
        return np.exp(-1j * (1 - a) * math.pi / 4) * ret[..., n_ - 1:3 * n_ - 2:2]

    eye = np.eye(n_, dtype=np.complex128)
    forward = chirp(eye, 0.5)
    shift = (np.arange(n_) + n_ // 2) % n_
    centred = (np.fft.ifft(eye[..., shift], axis=-1) * math.sqrt(n_))[..., np.argsort(shift)]
    return forward, chirp(centred, 0.5)


def pair(m):
    return np.concatenate([m.real, m.imag], 1), np.concatenate([-m.imag, m.real], 1)


def constant_tables():
    fwd, inv = frft_matrices()
    j = np.arange(128)
    turn = np.outer(j, j) % 128
    cos, sin = np.cos(2 * np.pi * turn / 128), np.sin(2 * np.pi * turn / 128)
    cos[turn % 64 == 32] = 0
    sin[turn % 64 == 0] = 0
    dft = cos - 1j * sin
    wgt = np.full(KW, 2.0)
    wgt[[0, KW - 1]] = 1.0
    tab = {}
    tab["frft_re"], tab["frft_im"] = pair(fwd)
    tab["ifrft_re"], tab["ifrft_im"] = pair(inv)
    tab["dft_h"] = pair(dft)[0]
    tab["dft_w_re"], tab["dft_w_im"] = pair(dft[:, :KW])
    tab["idft_h_re"], tab["idft_h_im"] = pair(np.conj(dft) / H)
    top = np.zeros((128, 128))
    top[:KW] = cos[:KW] * wgt[:, None] / W
    tab["idft_w_re"] = top
    top = np.zeros((128, 128))
    top[:KW] = -sin[:KW] * wgt[:, None] / W
    tab["idft_w_im"] = top
    tab["ident"] = np.eye(128)
    tab["average"] = np.full((128, 128), 1.0 / 128)
    tab["ones"] = np.ones((128, 128))
    rows = np.zeros((128, 2))
    rows[LO:LO + BOX, 0] = 1
    rows[:, 1] = 1 - rows[:, 0]
    tab["rows"] = rows
    for k in range(3):
        tab[f"band{k}"] = np.eye(128, k=1 - k)
    tab["lane"] = np.kron(np.eye(WB), np.ones((C0, 1)))
    for k in range(3):
        tab[f"tap{k}"] = np.kron(np.eye(WB, WO, k=-k), np.ones((C0, 1)))
    spread = np.zeros((128, 128))
    spread[:C0] = np.kron(np.ones((1, WB)), np.eye(C0))
    tab["spread"] = spread
    spread = np.zeros((128, 128))
    spread[:C1, :T] = np.kron(np.ones((1, 2)), np.eye(C1, C1 + 1))
    tab["spread2"] = spread
    lane2 = np.zeros((128, 2))
    lane2[:T] = np.kron(np.eye(2), np.ones((C1 + 1, 1)))
    tab["lane2"] = lane2
    lane12 = np.zeros((128, 2 * CG))
    lane12[[C1, 2 * C1 + 1]] = np.tile(np.eye(2), (1, CG))
    tab["lane12"] = lane12
    member = np.zeros((128, 2, G))
    for c in range(HALF):
        for h in range(2):
            member[c, h, (h * HALF + c) // CG] = 1
    tab["member"] = member.reshape(128, 2 * G)
    at, cols, start = {}, [], 0
    for name, t in tab.items():
        at[name] = (start, t.shape[1])
        cols.append(t)
        start += t.shape[1]
    return np.concatenate(cols, 1).astype(np.float32), at


def build(nc, x, tables, at, l0_w, l0_b, w1, w1_t, ws, ws_b, wf_in, wf_b, ww_t, ww_b,
          wp_t, wp_b, w0_t, w0_b, wc_t, wc_b, w2_t, out):
    f32 = mybir.dt.float32
    ALU = mybir.AluOpType
    ACT = mybir.ActivationFunctionType
    AX = mybir.AxisListType
    ctx = ExitStack()
    with ctx:
        def sb(name, shape):
            return ctx.enter_context(nc.sbuf_tensor(name, shape, f32))

        def sem(name):
            return ctx.enter_context(nc.semaphore(name))

        image = sb("image", [128, C, W])
        mix = sb("mix", [128, W, C1 + 1])
        work = sb("work", [128, 6, C0 * W])
        hop = sb("hop", [128, 4, 512])
        table = sb("table", [128, sum(k for _, k in at.values())])
        ps = ctx.enter_context(nc.psum_tensor("ps", [128, 8, 512], f32))

        def tab(name, rows=128):
            s, k = at[name]
            return table[0:rows, s:s + k]

        wraw0 = sb("wraw0", [128, 10])
        band = sb("band", [128, 3, 128])
        w1t_sb = sb("w1t_sb", [HALF, 2, C1])
        w1s = sb("w1s", [HALF, 2, C1])
        blk_s = sb("blk_s", [128, 3, C0 * WO])
        blk_f = sb("blk_f", [128, C0 * WB])
        blk_p = sb("blk_p", [128, C0 * WB])
        blk_c = sb("blk_c", [128, C0 * WB])
        blk_q = sb("blk_q", [128, C0 * WB])
        blk_o = sb("blk_o", [128, C, 2])
        blk_w2 = sb("blk_w2", [128, C, 2])
        bias_s = sb("bias_s", [128, C0])
        bias_f = sb("bias_f", [128, C0])
        bias_p = sb("bias_p", [128, C0])
        bias_c = sb("bias_c", [128, C0])
        bias_q = sb("bias_q", [128, C0])
        bias_0 = sb("bias_0", [128, C1])
        bias_1 = sb("bias_1", [128, C1])
        eps_t = sb("eps_t", [128, 1])
        half_pi = sb("half_pi", [128, 1])
        parts = sb("parts", [128, GQ, 12])
        xmv = sb("xmv", [128, 2, GQ, 2])
        ymv = sb("ymv", [128, G, 2])
        dev = sb("dev", [128, G])
        mean0 = sb("mean0", [128, G])
        nmean0 = sb("nmean0", [128, G])
        rstd0 = sb("rstd0", [128, G])
        mean1 = sb("mean1", [128, G])
        rstd1 = sb("rstd1", [128, G])
        tiny = sb("tiny", [128, G])
        prod = sb("prod", [HALF, 2, 2, G])
        col1 = sb("col1", [HALF, 2, 2])
        mrep = sb("mrep", [HALF, 2, 128])
        yparts = sb("yparts", [128, GQ, 12])
        scratch = sb("scratch", [128, 1])
        newt = sb("newt", [128, G])

        raw = work[:, 5, :]
        off = [0]

        def take(rows, cols):
            s = off[0]
            off[0] += cols
            return raw[0:rows, s:s + cols]

        r_ws = take(C0, C0 * 9)
        r_wf = take(C0, C0)
        r_ww = take(C0, C0)
        r_wp = take(C0, C0)
        r_w0 = take(C0, C0)
        r_wc = take(C0, C0)
        r_w1 = take(C0, C)
        r_w2 = take(C1, C)
        r_bs = take(C0, 1)
        r_bf = take(C0, 1)
        r_bw = take(128, C0)
        r_bp = take(128, C0)
        r_bc = take(128, C0)
        r_b0 = take(128, C0)
        r_bsr = take(C0, 128)
        r_bfr = take(C0, 128)
        r_sp = take(C0, C0 * 9)
        r_fp = take(C0, C0)
        s_exp = work[:, 4, 0:C0 * 9]
        f_exp = work[:, 4, 256:256 + C0]
        p_exp = work[:, 4, 272:272 + C0]
        c_exp = work[:, 4, 288:288 + C0]
        s_tmp = work[:, 4, 512:512 + C0 * WO]

        S = {k: sem(k) for k in (
            "weights_in", "setup_dve", "setup_pe", "ones_set",
            "x_parts", "x_mean", "x_dev", "x_var", "x_sd", "x_rstd", "centred", "conv", "y_out",
            "y_parts", "y_mean", "y_dev", "y_var", "y_sd", "mix_w", "mix_bias", "mix_ready",
            "y_turned", "turned_a", "turned_b", "mixed", "mix_out",
            "plane_1", "plane_1_out", "plane_2", "plane_2_out",
            "angle", "mag_turned", "pha_turned", "mag_turned_out", "pha_turned_out", "boxed",
            "box_turned", "box_turned_out", "mag_mixed", "mag_mixed_out", "pha_mixed", "pha_mixed_out",
            "box_mixed", "box_mixed_out", "polar", "back_1", "back_1_out", "back_2", "back_2_out",
            "abs_sum", "abs_done", "t_turned", "t_turned_act", "t_turned_dve", "final", "final_out", "link")}
        loaded = [sem(f"loaded{q}") for q in range(Q)]
        stored = [sem(f"stored{q}") for q in range(Q)]

        x_v = x.rearrange("n c h w -> n h c w")
        out_v = out.rearrange("n c h w -> n h c w")
        NW = 26

        def chunk(q):
            return slice(q * CQ, (q + 1) * CQ)

        def parts_of(q):
            step = CQ // LOADS
            return [slice(q * CQ + i * step, q * CQ + (i + 1) * step) for i in range(LOADS)]

        def group(g):
            return slice(g * CG, (g + 1) * CG)

        BR = [dict(k=0, first=2 * C0, cols=KW, t1=("dft_h", None), t2=("dft_w_re", "dft_w_im")),
              dict(k=1, first=C0, cols=W, t1=("frft_re", None), t2=("frft_re", "frft_im"))]
        for b in BR:
            b["starts"] = list(range(0, b["cols"] - WB + 1, WB))
            if b["starts"][-1] + WB < b["cols"]:
                b["starts"].append(b["cols"] - WB)
            b["banks"] = -(-len(b["starts"]) // 4)
        TB = sum(b["banks"] for b in BR)
        PAIRS = C0 // 2

        def spec(i, cols):
            return work[:, i, 0:C0 * cols].rearrange("p (w c) -> p c w", c=C0)

        block = ctx.enter_context(nc.Block())

        @block.sync
        def _(sp):
            for dst, src in ((table[:], tables[:]), (wraw0[:, 0:9], l0_w.broadcast_to([128, 9])), (wraw0[:, 9:10], l0_b.broadcast_to([128, 1])),
                             (w1t_sb[:], w1_t.rearrange("(s c) o -> c s o", s=2)),
                             (r_ws, ws), (r_wf, wf_in), (r_ww, ww_t), (r_wp, wp_t), (r_w0, w0_t), (r_wc, wc_t),
                             (r_w1, w1[0:C0, :]), (r_w2, w2_t), (r_bs, ws_b), (r_bf, wf_b),
                             (r_bw, ww_b.broadcast_to([128, C0])), (r_bp, wp_b.broadcast_to([128, C0])), (r_bc, wc_b.broadcast_to([128, C0])), (r_b0, w0_b.broadcast_to([128, C0]))):
                sp.dma_start(dst, src).then_inc(S["weights_in"], 16)
            for q in range(Q):
                for c in parts_of(q):
                    sp.dma_start(image[:, c, :], x_v[0, :, c, :]).then_inc(loaded[q], 16)
            with sp.Fori(0, N - 1) as n:
                for q in range(Q):
                    if q % 2 == 0:
                        sp.wait_ge(S["final_out"], n * 32 + 16 * (q // 2) + 16)
                    sp.dma_start(out_v[n, :, chunk(q), :], image[:, chunk(q), :]).then_inc(stored[q], 16)
                for q in range(Q):
                    sp.wait_ge(stored[q], n * 16 + 16)
                    for c in parts_of(q):
                        sp.dma_start(image[:, c, :], x_v[n + 1, :, c, :]).then_inc(loaded[q], 16)
            for q in range(Q):
                if q % 2 == 0:
                    sp.wait_ge(S["final_out"], (N - 1) * 32 + 16 * (q // 2) + 16)
                sp.dma_start(out_v[N - 1, :, chunk(q), :], image[:, chunk(q), :]).then_inc(stored[q], 16)
            for q in range(Q):
                sp.wait_ge(stored[q], N * 16)

        @block.tensor
        def _(pe):
            mm, turn = nc.tensor.matmul, nc.tensor.transpose
            ident = tab("ident")
            pe.wait_ge(S["setup_dve"], 1)
            for half in range(2):
                mm(ps[0:HALF, 0, half * C0:(half + 1) * C0], r_w1[:, half * HALF:(half + 1) * HALF], r_w0,
                   start=half == 0, stop=True, skip_group_check=True)
            for t in range(9):
                mm(ps[0:C0, 1, t * C0:(t + 1) * C0], r_ws.rearrange("o (c t) -> o t c", t=9)[:, t, :], r_ww,
                   start=t == 0, stop=True, skip_group_check=True)
            mm(ps[0:C0, 2, 0:C0], r_wf, r_ww, start=True, stop=True)
            mm(ps[:, 3, 0:C0], r_bsr, r_ww, start=True, stop=True)
            mm(ps[:, 4, 0:C0], r_bfr, r_ww, start=True, stop=True)
            mm(ps[0:T, 5, 0:C], tab("spread2", C1)[:, 0:T], r_w2, start=True, stop=True)
            mm(ps[:, 6, 0:C0], tab("spread", C0), r_wp, start=True, stop=True)
            mm(ps[:, 7, 0:C0], tab("spread", C0), r_wc, start=True, stop=True).then_inc(S["setup_pe"], 1)
            pe.wait_ge(S["setup_dve"], 2)
            mm(ps[:, 0, 0:C0 * 9], tab("spread", C0), r_sp, start=True, stop=True)
            mm(ps[:, 1, 0:C0], tab("spread", C0), r_fp, start=True, stop=True).then_inc(S["setup_pe"], 1)
            pe.wait_ge(S["setup_dve"], 3)

            def x_average(n, q):
                pe.wait_ge(S["x_parts"], n * Q + q + 1)
                mm(ps[:, 4, 0:GQ], tab("average"), xmv[:, q % 2, :, 0], start=True, stop=True)\
                    .then_inc(S["x_mean"], 1)

            def x_variance(n, q):
                pe.wait_ge(S["x_dev"], n * Q + q + 1)
                mm(ps[:, 5, 0:GQ], tab("average"), dev[:, 0:GQ], start=True, stop=True)\
                    .then_inc(S["x_var"], 1)

            def conv(n, g):
                pe.wait_ge(S["centred"], n * G + g + 1)
                if g >= 2:
                    pe.wait_ge(S["y_out"], n * G + g - 1)
                for j in range(2):
                    c = slice(g * CG + 3 * j, g * CG + 3 * j + 3)
                    o = ps[:, 2 * (g % 2) + j, 0:3 * W].rearrange("p (c w) -> p c w", c=3)
                    mm(o, band[:, 1, :], image[:, c, :], start=True, stop=False)
                    mm(o[:, :, 1:W], band[:, 0, :], image[:, c, 0:W - 1], start=False, stop=False)
                    last = mm(o[:, :, 0:W - 1], band[:, 2, :], image[:, c, 1:W], start=False, stop=True)
                last.then_inc(S["conv"], 1)

            with pe.Fori(0, N) as n:
                x_average(n, 0)
                x_variance(n, 0)
                for q in range(Q):
                    for g in range(GQ):
                        conv(n, q * GQ + g)
                        if q + 1 < Q and g == 1:
                            x_average(n, q + 1)
                        if q + 1 < Q and g == 4:
                            x_variance(n, q + 1)
                pe.wait_ge(S["y_parts"], n + 1)
                mm(ps[:, 4, 0:G], tab("average"), ymv[:, :, 0], start=True, stop=True).then_inc(S["y_mean"], 1)
                pe.wait_ge(S["y_dev"], n + 1)
                mm(ps[:, 5, 0:G], tab("average"), dev[:], start=True, stop=True).then_inc(S["y_var"], 1)
                pe.wait_ge(S["mix_w"], n + 1)
                for half in range(2):
                    last = mm(ps[:, 6, 0:C1], mrep[:, half, :], w1s[:, half, :], start=half == 0, stop=half == 1)
                last.then_inc(S["mix_bias"], 1)
                pe.wait_ge(S["mix_ready"], n + 1)

                def mix_block(b):
                    pe.wait_ge(S["turned_a"], n * 32 + b + 1)
                    pe.wait_ge(S["turned_b"], n * 32 + b + 1)
                    if b % 2 == 0 and b >= 4:
                        pe.wait_ge(S["mix_out"], n * 16 + b // 2 - 1)
                    for i in range(4):
                        o = ps[:, (b // 2) % 2, ((b % 2) * 4 + i) * C1:((b % 2) * 4 + i + 1) * C1]
                        for half in range(2):
                            last = mm(o, hop[0:HALF, 2 * (b % 2) + half, i * 128:(i + 1) * 128], w1s[:, half, :],
                                      start=half == 0, stop=half == 1)
                    last.then_inc(S["mixed"], 1)

                for b in range(32):
                    if b >= 2:
                        pe.wait_ge(S["turned_a"], n * 32 + b - 1)
                        pe.wait_ge(S["turned_b"], n * 32 + b - 1)
                    for half in range(2):
                        for i in range(4):
                            last = turn(ps[0:HALF, 4 + 2 * (b % 2) + half, i * 128:(i + 1) * 128],
                                        image[:, half * HALF:(half + 1) * HALF, 4 * b + i], ident)
                    last.then_inc(S["y_turned"], 1)
                    if b >= 1:
                        mix_block(b - 1)
                mix_block(31)
                pe.wait_ge(S["mix_out"], n * 16 + 16)

                for br in BR:
                    k, cols = br["k"], br["cols"]

                    def plane_2(p):
                        pe.wait_ge(S["plane_1_out"], n * 2 * PAIRS + k * PAIRS + p + 1)
                        if p >= 2:
                            pe.wait_ge(S["plane_2_out"], n * 2 * PAIRS + k * PAIRS + p - 1)
                        for i in range(2):
                            o = ps[:, 2 + p % 2, i * 2 * cols:(i + 1) * 2 * cols]
                            a = hop[:, p % 2, i * 256:(i + 1) * 256]
                            mm(o, a[:, 0:128], tab(br["t2"][0]), start=True, stop=False)
                            last = mm(o, a[:, 128:256], tab(br["t2"][1]), start=False, stop=True)
                        last.then_inc(S["plane_2"], 1)

                    for p in range(PAIRS):
                        if p >= 2:
                            pe.wait_ge(S["plane_1_out"], n * 2 * PAIRS + k * PAIRS + p - 1)
                        for i in range(2):
                            last = mm(ps[:, p % 2, i * 256:(i + 1) * 256], mix[:, :, br["first"] + 2 * p + i],
                                      tab(br["t1"][0]), start=True, stop=True)
                        last.then_inc(S["plane_1"], 1)
                        if p >= 1:
                            plane_2(p - 1)
                    plane_2(PAIRS - 1)

                    base = n * TB + k * BR[0]["banks"]
                    pe.wait_ge(S["angle"], n * 28 + k * 14 + 14)
                    for m, (src, sent, gone) in enumerate(((2, "mag_turned", "mag_turned_out"),
                                                           (3, "pha_turned", "pha_turned_out"))):
                        for t in range(br["banks"]):
                            if t >= 2:
                                pe.wait_ge(S[gone], base + t - 1)
                            some = br["starts"][4 * t:4 * t + 4]
                            for i, s in enumerate(some):
                                last = turn(ps[:, 4 + 2 * m + t % 2, i * 128:(i + 1) * 128],
                                            work[:, src, C0 * s:C0 * (s + WB)], ident)
                            last.then_inc(S[sent], 1)
                    if k:
                        pe.wait_ge(S["boxed"], n + 1)
                        for t in range(4):
                            if t >= 2:
                                pe.wait_ge(S["box_turned_out"], n * 4 + t - 1)
                            for i, j in enumerate(range(4 * t, min(4 * t + 4, NBOX))):
                                last = turn(ps[:, t % 2, i * 128:(i + 1) * 128], work[:, 4, C0 * WO * j:C0 * (WO * j + WB)], ident)
                            last.then_inc(S["box_turned"], 1)
                    pe.wait_ge(S["mag_turned_out"], base + br["banks"])
                    pe.wait_ge(S["pha_turned_out"], base + br["banks"])
                    for m, (weights, sent, gone) in enumerate(
                            ((blk_f if k else blk_c, "mag_mixed", "mag_mixed_out"),
                             (blk_p if k else blk_q, "pha_mixed", "pha_mixed_out"))):
                        for t in range(br["banks"]):
                            if t >= 2:
                                pe.wait_ge(S[gone], base + t - 1)
                            for i in range(len(br["starts"][4 * t:4 * t + 4])):
                                j = 4 * t + i
                                last = mm(ps[:, 4 + 2 * m + t % 2, i * 128:(i + 1) * 128],
                                          work[:, m, j * 128:(j + 1) * 128], weights[:], start=True, stop=True)
                            last.then_inc(S[sent], 1)
                    if k:
                        pe.wait_ge(S["box_turned_out"], n * 4 + 4)
                        boxed = work[:, 5, 0:NBOX * 130].rearrange("p (j h) -> p j h", j=NBOX)
                        for t in range(3):
                            for i in range(5):
                                o = ps[:, 1 + t, i * C0 * WO:(i + 1) * C0 * WO]
                                for dy in range(3):
                                    last = mm(o, boxed[:, 5 * t + i, dy:dy + 128], blk_s[:, dy, :],
                                              start=dy == 0, stop=dy == 2)
                            last.then_inc(S["box_mixed"], 1)

                    pe.wait_ge(S["polar"], n * 14 + k * 7 + 7)
                    pa = n * 2 * PAIRS + k * PAIRS

                    def back_2(p):
                        pe.wait_ge(S["back_1_out"], pa + p + 1)
                        if p >= 2:
                            pe.wait_ge(S["back_2_out"], pa + p - 1)
                        for i in range(2):
                            a = hop[0:cols, p % 2, i * 256:(i + 1) * 256]
                            o = ps[:, 2 + p % 2, i * 256:(i + 1) * 256] if k else ps[:, 2 + p % 2, i * 128:(i + 1) * 128]
                            re, im = ("ifrft_re", "ifrft_im") if k else ("idft_w_re", "idft_w_im")
                            mm(o, a[:, 0:128], tab(re, cols), start=True, stop=False)
                            last = mm(o, a[:, 128:256], tab(im, cols), start=False, stop=True)
                        last.then_inc(S["back_2"], 1)

                    re, im = ("ifrft_re", "ifrft_im") if k else ("idft_h_re", "idft_h_im")
                    for p in range(PAIRS):
                        if p >= 2:
                            pe.wait_ge(S["back_1_out"], pa + p - 1)
                        for i in range(2):
                            o = ps[0:cols, p % 2, i * 256:(i + 1) * 256]
                            mm(o, spec(0, cols)[:, 2 * p + i, :], tab(re), start=True, stop=False)
                            last = mm(o, spec(1, cols)[:, 2 * p + i, :], tab(im), start=False, stop=True)
                        last.then_inc(S["back_1"], 1)
                        if p >= 1:
                            back_2(p - 1)
                    back_2(PAIRS - 1)
                    pe.wait_ge(S["back_2_out"], pa + PAIRS)

                pe.wait_ge(S["abs_done"], n + 1)
                for t in range(16):
                    if t >= 4:
                        pe.wait_ge(S["t_turned_act" if t % 2 == 0 else "t_turned_dve"], n * 8 + t // 2 - 1)
                    for i in range(4):
                        j = 4 * t + i
                        last = turn(ps[0:T, t % 4, i * 128:(i + 1) * 128], mix[:, 2 * j:2 * j + 2, :], ident)
                    last.then_inc(S["t_turned"], 1)
                pe.wait_ge(S["t_turned_act"], n * 8 + 8)
                pe.wait_ge(S["t_turned_dve"], n * 8 + 8)
                planes = work[:, 0:4, :].rearrange("p a (b h) -> p (a b) h", h=128)
                for u in range(32):
                    half, v = u // 16, u % 16
                    if u >= 4:
                        pe.wait_ge(S["final_out"], n * 32 + u - 3)
                    for bank in range(2):
                        for i in range(2):
                            o = ps[:, 2 * (u % 4) + bank, 0:4 * HALF].rearrange("p (c w) -> p c w", w=4)
                            last = mm(o[:, :, 2 * i:2 * i + 2], planes[0:T, 4 * v + 2 * bank + i, :],
                                      blk_o[0:T, half * HALF:(half + 1) * HALF, :],
                                      start=i == 0, stop=True, skip_group_check=True)
                    last.then_inc(S["final"], 1)

        @block.scalar
        def _(act):
            act.wait_ge(S["setup_dve"], 3)
            with act.Fori(0, N) as n:
                def centre(g):
                    nc.scalar.activation(image[:, group(g), :], image[:, group(g), :], ACT.Identity,
                                         bias=nmean0[:, g:g + 1]).then_inc(S["centred"], 1)

                def x_sd(q):
                    act.wait_ge(S["x_var"], n * Q + q + 1)
                    nc.scalar.activation(tiny[:, 0:GQ], ps[:, 5, 0:GQ], ACT.Sqrt, bias=eps_t[:]).then_inc(S["x_sd"], 1)

                x_sd(0)
                for q in range(Q):
                    act.wait_ge(S["x_rstd"], n * Q + q + 1)
                    for g in range(GQ):
                        centre(q * GQ + g)
                    if q + 1 < Q:
                        x_sd(q + 1)
                act.wait_ge(S["y_var"], n + 1)
                nc.scalar.activation(tiny[:], ps[:, 5, 0:G], ACT.Sqrt, bias=eps_t[:]).then_inc(S["y_sd"], 1)
                for b in range(32):
                    act.wait_ge(S["y_turned"], n * 32 + b + 1)
                    if b >= 2:
                        act.wait_ge(S["mixed"], n * 32 + b - 1)
                    nc.scalar.copy(hop[0:HALF, 2 * (b % 2), :], ps[0:HALF, 4 + 2 * (b % 2), :]).then_inc(S["turned_a"], 1)
                act.wait_ge(S["mixed"], n * 32 + 32)
                for br in BR:
                    k, cols = br["k"], br["cols"]
                    size = C0 * cols
                    pa = n * 2 * PAIRS + k * PAIRS
                    for p in range(PAIRS):
                        act.wait_ge(S["plane_1"], pa + p + 1)
                        if p >= 2:
                            act.wait_ge(S["plane_2"], pa + p - 1)
                        nc.scalar.copy(hop[:, p % 2, :], ps[:, p % 2, :]).then_inc(S["plane_1_out"], 1)
                    buf = [work[:, i, 0:size] for i in range(6)]
                    act.wait_ge(S["plane_2_out"], pa + PAIRS)
                    nc.scalar.activation(buf[4], buf[0], ACT.Square).then_inc(S["angle"], 1)
                    nc.scalar.activation(buf[5], buf[1], ACT.Square).then_inc(S["angle"], 1)
                    a0 = n * 28 + k * 14
                    act.wait_ge(S["angle"], a0 + 3)
                    nc.scalar.activation(buf[2], buf[4], ACT.Sqrt).then_inc(S["angle"], 1)
                    nc.scalar.activation(buf[5], buf[0], ACT.Abs).then_inc(S["angle"], 1)
                    act.wait_ge(S["angle"], a0 + 8)
                    nc.scalar.activation(buf[3], buf[5], ACT.Arctan).then_inc(S["angle"], 1)
                    base = n * TB + k * BR[0]["banks"]
                    for t in range(br["banks"]):
                        act.wait_ge(S["mag_turned"], base + t + 1)
                        u = len(br["starts"][4 * t:4 * t + 4]) * 128
                        nc.scalar.copy(work[:, 0, 512 * t:512 * t + u], ps[:, 4 + t % 2, 0:u])\
                            .then_inc(S["mag_turned_out"], 1)
                    c0 = n * 14 + k * 7
                    act.wait_ge(S["polar"], c0 + 2)
                    nc.scalar.activation(buf[5], buf[4], ACT.Sin, scale=TWO_PI).then_inc(S["polar"], 1)
                    nc.scalar.activation(buf[3], buf[4], ACT.Abs).then_inc(S["polar"], 1)
                    act.wait_ge(S["polar"], c0 + 4)
                    nc.scalar.activation(buf[3], buf[3], ACT.Sin, scale=-TWO_PI, bias=half_pi[:]).then_inc(S["polar"], 1)
                    for p in range(PAIRS):
                        act.wait_ge(S["back_1"], pa + p + 1)
                        if p >= 2:
                            act.wait_ge(S["back_2"], pa + p - 1)
                        nc.scalar.copy(hop[0:cols, p % 2, :], ps[0:cols, p % 2, :]).then_inc(S["back_1_out"], 1)
                        if k and p >= 1:
                            act.wait_ge(S["back_2"], pa + p)
                            if p >= 3:
                                act.wait_ge(S["abs_sum"], n * PAIRS + p - 2)
                            nc.scalar.activation(hop[:, 2 + (p - 1) % 2, :], ps[:, 2 + (p - 1) % 2, :], ACT.Square)\
                                .then_inc(S["back_2_out"], 1)
                    if k:
                        act.wait_ge(S["back_2"], pa + PAIRS)
                        act.wait_ge(S["abs_sum"], n * PAIRS + PAIRS - 2)
                        nc.scalar.activation(hop[:, 2 + (PAIRS - 1) % 2, :], ps[:, 2 + (PAIRS - 1) % 2, :], ACT.Square)\
                            .then_inc(S["back_2_out"], 1)
                        act.wait_ge(S["abs_sum"], n * PAIRS + PAIRS)
                        nc.scalar.activation(mix[:, :, C0:2 * C0], buf[4].rearrange("p (c w) -> p w c", c=C0), ACT.Sqrt)\
                            .then_inc(S["abs_done"], 1)
                for t in range(0, 16, 2):
                    act.wait_ge(S["t_turned"], n * 16 + t + 1)
                    nc.scalar.copy(work[0:T, t // 4, 512 * (t % 4):512 * (t % 4) + 512], ps[0:T, t % 4, :])\
                        .then_inc(S["t_turned_act"], 1)

        @block.gpsimd
        def _(pool):
            pool.memset(mix[:, :, C1:C1 + 1], 1.0).then_inc(S["ones_set"], 1)
            with pool.Fori(0, N) as n:
                for br in BR:
                    k, cols = br["k"], br["cols"]
                    size = C0 * cols
                    buf = [work[:, i, 0:size] for i in range(6)]
                    a0 = n * 28 + k * 14
                    pool.wait_ge(S["angle"], a0 + 2)
                    nc.gpsimd.tensor_tensor(buf[4], buf[4], buf[5], ALU.add).then_inc(S["angle"], 1)
                    pool.wait_ge(S["angle"], a0 + 7)
                    nc.gpsimd.tensor_tensor(buf[5], buf[1], buf[5], ALU.mult).then_inc(S["angle"], 1)
                    c0 = n * 14 + k * 7
                    pool.wait_ge(S["polar"], c0 + 1)
                    nc.gpsimd.tensor_tensor(buf[4], buf[3], buf[4], ALU.subtract).then_inc(S["polar"], 1)
                    pool.wait_ge(S["polar"], c0 + 5)
                    nc.gpsimd.tensor_tensor(buf[1], buf[2], buf[5], ALU.mult).then_inc(S["polar"], 1)
                    if k:
                        for p in range(PAIRS):
                            pool.wait_ge(S["back_2_out"], n * 2 * PAIRS + PAIRS + p + 1)
                            v = hop[:, 2 + p % 2, :].rearrange("p (c r w) -> p c r w", c=2, r=2)
                            nc.gpsimd.tensor_tensor(buf[4][:, p * 256:(p + 1) * 256].rearrange("p (c w) -> p c w", c=2),
                                                    v[:, :, 0, :], v[:, :, 1, :], ALU.add).then_inc(S["abs_sum"], 1)

        @block.vector
        def _(dve):
            v = nc.vector
            linked = [0, None, 0]

            def link(ins):
                linked[0] += 1
                ins.then_inc(S["link"], 1)
                value = linked[0]
                if linked[1] is not None:
                    value = linked[1] * LINKS + value
                dve.wait_ge(S["link"], value)

            v.memset(eps_t[:], EPS)
            v.memset(half_pi[:], math.pi / 2)
            v.memset(bias_0[:], 0.0)
            dve.wait_ge(S["weights_in"], 18 * 16)
            v.tensor_scalar(r_bsr, tab("ones", C0), r_bs, None, ALU.mult)
            v.tensor_scalar(r_bfr, tab("ones", C0), r_bf, None, ALU.mult).then_inc(S["setup_dve"], 1)
            for kx in range(3):
                link(v.tensor_scalar(band[:, kx, :], tab("band0"), wraw0[:, kx:kx + 1], None, ALU.mult))
                for ky in (1, 2):
                    link(v.scalar_tensor_tensor(band[:, kx, :], tab(f"band{ky}"), wraw0[:, 3 * ky + kx:3 * ky + kx + 1],
                                                band[:, kx, :], ALU.mult, ALU.add))
            dve.wait_ge(S["setup_pe"], 1)
            v.tensor_copy(w1t_sb[:, :, 0:C0], ps[0:HALF, 0, 0:2 * C0].rearrange("p (s o) -> p s o", s=2))
            v.tensor_copy(r_sp, ps[0:C0, 1, 0:9 * C0])
            v.tensor_copy(r_fp, ps[0:C0, 2, 0:C0])
            v.tensor_tensor(bias_s[:], ps[:, 3, 0:C0], r_bw, ALU.add)
            v.tensor_tensor(bias_f[:], ps[:, 4, 0:C0], r_bw, ALU.add)
            v.tensor_copy(p_exp, ps[:, 6, 0:C0])
            v.tensor_copy(c_exp, ps[:, 7, 0:C0])
            v.tensor_copy(bias_c[:], r_bc)
            v.tensor_copy(bias_0[:, 0:C0], r_b0)
            v.tensor_scalar(bias_p[:], r_bp, 1 / (2 * math.pi), None, ALU.mult)
            v.tensor_scalar(bias_q[:], r_bc, 1 / (2 * math.pi), None, ALU.mult)
            link(v.tensor_tensor(blk_w2[0:T], ps[0:T, 5, 0:C].rearrange("p (c w) -> p c w", w=1).broadcast_to([T, C, 2]),
                                 tab("lane2", T).rearrange("p (c w) -> p c w", c=1).broadcast_to([T, C, 2]), ALU.mult))
            v.memset(dev[:, 0:1], 0.0).then_inc(S["setup_dve"], 1)
            dve.wait_ge(S["setup_pe"], 2)
            v.tensor_copy(s_exp, ps[:, 0, 0:9 * C0])
            link(v.tensor_copy(f_exp, ps[:, 1, 0:C0]))

            def spread(dst, src, mask, w):
                return v.tensor_tensor(dst.rearrange("p (b o) -> p b o", b=w),
                                       src.rearrange("p (b o) -> p b o", b=1).broadcast_to([128, w, C0]),
                                       mask.rearrange("p (b o) -> p b o", o=1).broadcast_to([128, w, C0]), ALU.mult)

            link(spread(blk_f[:], f_exp, tab("lane"), WB))
            link(spread(blk_c[:], c_exp, tab("lane"), WB))
            link(spread(blk_p[:], p_exp, tab("lane"), WB))
            link(v.tensor_scalar(blk_p[:], blk_p[:], 2 / math.pi, None, ALU.mult))
            link(v.tensor_scalar(blk_q[:], blk_c[:], 2 / math.pi, None, ALU.mult))
            for ky in range(3):
                link(spread(blk_s[:, ky, :], s_exp[:, 3 * ky * C0:(3 * ky + 1) * C0], tab("tap0"), WO))
                for kx in (1, 2):
                    link(spread(s_tmp, s_exp[:, (3 * ky + kx) * C0:(3 * ky + kx + 1) * C0], tab(f"tap{kx}"), WO))
                    link(v.tensor_tensor(blk_s[:, ky, :], blk_s[:, ky, :], s_tmp, ALU.add))
            dve.wait_ge(S["ones_set"], 1)
            v.memset(dev[:, 0:1], 0.0).then_inc(S["setup_dve"], 1)

            LINKS = 45
            SETUP_LINKS = linked[0]
            def newton(dst, sd, var, k):
                t = newt[:, 0:k]
                link(v.reciprocal(dst, sd))
                link(v.tensor_tensor(t, dst, dst, ALU.mult))
                link(v.scalar_tensor_tensor(t, var, EPS, t, ALU.add, ALU.mult))
                link(v.tensor_scalar(t, t, -0.5, 1.5, ALU.mult, ALU.add))
                return v.tensor_tensor(dst, dst, t, ALU.mult)

            with dve.Fori(0, N) as n:
                linked[1] = n

                def x_parts(q):
                    dve.wait_ge(loaded[q], n * 16 * LOADS + 16 * LOADS)
                    for g in range(GQ):
                        for j in range(2):
                            c = (q * GQ + g) * CG + 3 * j
                            last = v.bn_stats(parts[:, g, 6 * j:6 * j + 6], image[:, c:c + 3, :])
                    link(last)
                    v.memset(scratch[:], 0.0)
                    for g in range(GQ):
                        last = v.bn_aggr(xmv[:, q % 2, g, :], parts[:, g, :])
                    last.then_inc(S["x_parts"], 1)

                def x_dev(q):
                    gs = slice(q * GQ, (q + 1) * GQ)
                    dve.wait_ge(S["x_mean"], n * Q + q + 1)
                    v.tensor_copy(mean0[:, gs], ps[:, 4, 0:GQ])
                    v.tensor_scalar(nmean0[:, gs], ps[:, 4, 0:GQ], -1.0, None, ALU.mult)
                    link(v.tensor_tensor(dev[:, 0:GQ], xmv[:, q % 2, :, 0], ps[:, 4, 0:GQ], ALU.subtract))
                    link(v.tensor_tensor(dev[:, 0:GQ], dev[:, 0:GQ], dev[:, 0:GQ], ALU.mult))
                    v.tensor_tensor(dev[:, 0:GQ], dev[:, 0:GQ], xmv[:, q % 2, :, 1], ALU.add).then_inc(S["x_dev"], 1)

                def x_rstd(q):
                    gs = slice(q * GQ, (q + 1) * GQ)
                    dve.wait_ge(S["x_sd"], n * Q + q + 1)
                    newton(rstd0[:, gs], tiny[:, 0:GQ], ps[:, 5, 0:GQ], GQ).then_inc(S["x_rstd"], 1)

                x_parts(0)
                x_dev(0)
                x_rstd(0)
                dve.wait_ge(S["x_rstd"], n * Q + 1)
                for q in range(Q):
                    if q + 1 < Q:
                        x_parts(q + 1)
                    for i in range(GQ):
                        g = q * GQ + i
                        dve.wait_ge(S["conv"], n * G + g + 1)
                        o = ps[:, 2 * (g % 2):2 * (g % 2) + 2, 0:3 * W]
                        y = image[:, group(g), :].rearrange("p (a c) w -> p a (c w)", a=2)
                        v.scalar_tensor_tensor(y, o, rstd0[:, g:g + 1], y, ALU.mult, ALU.add).then_inc(S["y_out"], 1)
                        dve.wait_ge(S["y_out"], n * G + g + 1)
                        for j in range(2):
                            last = v.bn_stats(yparts[:, i, 6 * j:6 * j + 6], image[:, g * CG + 3 * j:g * CG + 3 * j + 3, :])
                        if q + 1 < Q and i == 2:
                            x_dev(q + 1)
                        if q + 1 < Q and i == 5:
                            x_rstd(q + 1)
                    link(last)
                    v.memset(scratch[:], 0.0)
                    for i in range(GQ):
                        last = v.bn_aggr(ymv[:, q * GQ + i, :], yparts[:, i, :])
                last.then_inc(S["y_parts"], 1)
                dve.wait_ge(S["y_mean"], n + 1)
                v.tensor_copy(mean1[:], ps[:, 4, 0:G])
                link(v.tensor_tensor(dev[:], ymv[:, :, 0], ps[:, 4, 0:G], ALU.subtract))
                link(v.tensor_tensor(dev[:], dev[:], dev[:], ALU.mult))
                v.tensor_tensor(dev[:], dev[:], ymv[:, :, 1], ALU.add).then_inc(S["y_dev"], 1)
                dve.wait_ge(S["y_sd"], n + 1)
                link(newton(rstd1[:], tiny[:], ps[:, 5, 0:G], G))
                member = tab("member", HALF).rearrange("p (s g) -> p s g", s=2)
                for j, src in enumerate((rstd1, mean1)):
                    last = v.tensor_tensor(prod[:, j], member,
                                           src[0:HALF].rearrange("p (s g) -> p s g", s=1).broadcast_to([HALF, 2, G]), ALU.mult)
                link(last)
                link(v.tensor_reduce(col1[:].rearrange("p a b -> p (a b)"), prod[:].rearrange("p a b g -> p (a b) g"), AX.X, ALU.add))
                for half in range(2):
                    v.tensor_scalar(w1s[:, half, :], w1t_sb[:, half, :], col1[:, 0, half:half + 1], None, ALU.mult)
                    last = v.tensor_scalar(mrep[:, half, :], tab("ones", HALF), col1[:, 1, half:half + 1], None, ALU.mult)
                last.then_inc(S["mix_w"], 1)
                dve.wait_ge(S["mix_bias"], n + 1)
                v.tensor_tensor(bias_1[:], bias_0[:], ps[:, 6, 0:C1], ALU.subtract)
                link(v.tensor_scalar(tiny[:], mean0[:], wraw0[:, 9:10], None, ALU.add))
                link(v.tensor_tensor(blk_o[0:T].rearrange("p (g c) w -> p g (c w)", g=G),
                                     tiny[0:T].rearrange("p (g c) -> p g c", c=1).broadcast_to([T, G, 2 * CG]),
                                     tab("lane12", T).rearrange("p (g c) -> p g c", g=1).broadcast_to([T, G, 2 * CG]),
                                     ALU.mult))
                v.tensor_tensor(blk_o[0:T], blk_o[0:T], blk_w2[0:T], ALU.add).then_inc(S["mix_ready"], 1)
                dve.wait_ge(S["mix_ready"], n + 1)

                def mix_out(u):
                    dve.wait_ge(S["mixed"], n * 32 + 2 * u + 2)
                    v.tensor_tensor(mix[:, 8 * u:8 * u + 8, 0:C1],
                                    ps[:, u % 2, 0:8 * C1].rearrange("p (w o) -> p w o", w=8),
                                    bias_1[:].rearrange("p (w o) -> p w o", w=1).broadcast_to([128, 8, C1]), ALU.add)\
                        .then_inc(S["mix_out"], 1)

                for b in range(32):
                    dve.wait_ge(S["y_turned"], n * 32 + b + 1)
                    if b >= 2:
                        dve.wait_ge(S["mixed"], n * 32 + b - 1)
                    v.tensor_copy(hop[0:HALF, 2 * (b % 2) + 1, :], ps[0:HALF, 5 + 2 * (b % 2), :]).then_inc(S["turned_b"], 1)
                    if b >= 3 and b % 2:
                        mix_out((b - 3) // 2)
                mix_out(15)

                for br in BR:
                    k, cols = br["k"], br["cols"]
                    size = C0 * cols
                    buf = [work[:, i, 0:size] for i in range(6)]
                    pa = n * 2 * PAIRS + k * PAIRS
                    for p in range(PAIRS):
                        dve.wait_ge(S["plane_2"], pa + p + 1)
                        v.tensor_copy(work[:, 0:2, 0:size].rearrange("p r (w c) -> p r c w", c=C0)[:, :, 2 * p:2 * p + 2, :],
                                      ps[:, 2 + p % 2, 0:4 * cols].rearrange("p (c r w) -> p r c w", c=2, r=2))\
                            .then_inc(S["plane_2_out"], 1)
                    a0 = n * 28 + k * 14
                    dve.wait_ge(S["angle"], a0 + 5)
                    v.scalar_tensor_tensor(buf[4], buf[2], 1e-30, buf[5], ALU.max, ALU.add).then_inc(S["angle"], 1)
                    dve.wait_ge(S["angle"], a0 + 6)
                    v.reciprocal(buf[5], buf[4]).then_inc(S["angle"], 1)
                    dve.wait_ge(S["angle"], a0 + 9)
                    v.tensor_scalar(buf[4], buf[1], 0.0, 0.5, ALU.is_ge, ALU.subtract).then_inc(S["angle"], 1)
                    v.tensor_scalar(buf[5], buf[0], 0.0, 0.5, ALU.is_ge, ALU.subtract).then_inc(S["angle"], 1)
                    dve.wait_ge(S["angle"], a0 + 11)
                    v.scalar_tensor_tensor(buf[3], buf[4], -math.pi / 2, buf[3], ALU.mult, ALU.add).then_inc(S["angle"], 1)
                    dve.wait_ge(S["angle"], a0 + 12)
                    v.tensor_tensor(buf[3], buf[3], buf[5], ALU.mult).then_inc(S["angle"], 1)
                    dve.wait_ge(S["angle"], a0 + 13)
                    v.scalar_tensor_tensor(buf[3], buf[4], math.pi / 4, buf[3], ALU.mult, ALU.add).then_inc(S["angle"], 1)
                    base = n * TB + k * BR[0]["banks"]
                    if k:
                        dve.wait_ge(S["angle"], a0 + 14)
                        box = work[:, 4, 0:C0 * (BOX + 2)]
                        v.memset(box[:, 0:C0], 0.0)
                        v.memset(box[:, C0 * (BOX + 1):], 0.0)
                        v.tensor_scalar(box[:, C0:C0 * (BOX + 1)], work[:, 2, C0 * LO:C0 * (LO + BOX)], tab("rows")[:, 0:1],
                                        None, ALU.mult).then_inc(S["boxed"], 1)
                    for t in range(br["banks"]):
                        dve.wait_ge(S["pha_turned"], base + t + 1)
                        u = len(br["starts"][4 * t:4 * t + 4]) * 128
                        v.tensor_copy(work[:, 1, 512 * t:512 * t + u], ps[:, 6 + t % 2, 0:u])\
                            .then_inc(S["pha_turned_out"], 1)
                    if k:
                        boxed = work[:, 5, 0:NBOX * 130].rearrange("p (j h) -> p j h", j=NBOX)
                        v.memset(boxed[:, :, 0], 0.0)
                        v.memset(boxed[:, :, 129], 0.0)
                        for t in range(4):
                            m = min(4, NBOX - 4 * t)
                            dve.wait_ge(S["box_turned"], n * 4 + t + 1)
                            v.tensor_copy(boxed[:, 4 * t:4 * t + m, 1:129],
                                          ps[:, t % 2, 0:m * 128].rearrange("p (j h) -> p j h", j=m))\
                                .then_inc(S["box_turned_out"], 1)

                    def mixed_out(dst, sent, gone, bank, bias):
                        for t in range(br["banks"]):
                            some = br["starts"][4 * t:4 * t + 4]
                            m = len(some)
                            dve.wait_ge(S[sent], base + t + 1)
                            assert some[-1] - some[0] == WB * (m - 1)
                            skip = 4 * t * WB - some[0]
                            fresh = m * WB - skip
                            o = work[:, dst, C0 * 4 * t * WB:C0 * (4 * t * WB + fresh)].rearrange("p (w o) -> p w o", o=C0)
                            i = ps[:, bank + t % 2, C0 * skip:m * 128].rearrange("p (w o) -> p w o", o=C0)
                            z = bias[:].rearrange("p (w o) -> p w o", w=1).broadcast_to([128, fresh, C0])
                            v.tensor_tensor(o, i, z, ALU.add).then_inc(S[gone], 1)

                    mixed_out(2, "mag_mixed", "mag_mixed_out", 4, bias_f if k else bias_c)
                    mixed_out(3, "pha_mixed", "pha_mixed_out", 6, bias_p if k else bias_q)
                    if k:
                        inner = work[:, 2, C0 * LO:C0 * (LO + BOX)]
                        dve.wait_ge(S["mag_mixed_out"], base + br["banks"])
                        link(v.tensor_scalar(inner, inner, tab("rows")[:, 1:2], None, ALU.mult))
                        conv_s = work[:, 4, 0:C0 * BOX]
                        for t in range(3):
                            dve.wait_ge(S["box_mixed"], n * 3 + t + 1)
                            v.tensor_tensor(conv_s[:, 480 * t:480 * t + 480].rearrange("p (w o) -> p w o", o=C0),
                                            ps[:, 1 + t, 0:480].rearrange("p (w o) -> p w o", o=C0),
                                            bias_s[:].rearrange("p (w o) -> p w o", w=1).broadcast_to([128, 30, C0]),
                                            ALU.add).then_inc(S["box_mixed_out"], 1)
                        dve.wait_ge(S["box_mixed_out"], n * 3 + 3)
                        link(v.scalar_tensor_tensor(inner, conv_s, tab("rows")[:, 0:1], inner, ALU.mult, ALU.add))
                    c0 = n * 14 + k * 7
                    dve.wait_ge(S["pha_mixed_out"], base + br["banks"])
                    v.tensor_scalar(buf[4], buf[3], ROUND, ROUND, ALU.add, ALU.subtract).then_inc(S["polar"], 1)
                    dve.wait_ge(S["polar"], c0 + 6)
                    v.tensor_tensor(buf[0], buf[2], buf[3], ALU.mult).then_inc(S["polar"], 1)
                    if not k:
                        for p in range(PAIRS):
                            dve.wait_ge(S["back_2"], pa + p + 1)
                            v.tensor_copy(mix[:, :, 2 * C0 + 2 * p:2 * C0 + 2 * p + 2].rearrange("p w c -> p c w"),
                                          ps[:, 2 + p % 2, 0:256].rearrange("p (c w) -> p c w", c=2))\
                                .then_inc(S["back_2_out"], 1)
                for t in range(1, 16, 2):
                    dve.wait_ge(S["t_turned"], n * 16 + t + 1)
                    v.tensor_copy(work[0:T, t // 4, 512 * (t % 4):512 * (t % 4) + 512], ps[0:T, t % 4, :])\
                        .then_inc(S["t_turned_dve"], 1)
                for u in range(32):
                    half, w = u // 16, u % 16
                    dve.wait_ge(S["final"], n * 32 + u + 1)
                    y = image[:, half * HALF:(half + 1) * HALF, 8 * w:8 * w + 8].rearrange("p c (b w) -> p b c w", b=2)
                    o = ps[:, 2 * (u % 4):2 * (u % 4) + 2, 0:4 * HALF].rearrange("p b (c w) -> p b c w", w=4)
                    v.tensor_tensor(y, y, o, ALU.add).then_inc(S["final_out"], 1)
            assert linked[0] - SETUP_LINKS == LINKS, linked[0] - SETUP_LINKS


def kernel(x, L0_conv_w, L0_conv_b, L1_conv_conv1_w, L1_conv_mag_s_w, L1_conv_mag_s_b, L1_conv_mag_f_w,
           L1_conv_mag_f_b, L1_conv_mag_w, L1_conv_mag_b, L1_conv_pha_w, L1_conv_pha_b, L1_conv_conv_0_w,
           L1_conv_conv_0_b, L1_conv_conv_1_w, L1_conv_conv_1_b, L1_conv_conv2_w):
    import concourse.bacc as bacc
    from concourse.bass_utils import run_bass_kernel_spmd

    tables, at = constant_tables()
    row = lambda a: np.ascontiguousarray(a).reshape(1, -1)
    col = lambda a: np.ascontiguousarray(a).reshape(-1, 1)
    turned = lambda a: np.ascontiguousarray(np.asarray(a).T)
    arrays = dict(
        x=np.ascontiguousarray(x), tables=tables, l0_w=row(L0_conv_w), l0_b=row(L0_conv_b),
        w1=np.ascontiguousarray(L1_conv_conv1_w), w1_t=turned(L1_conv_conv1_w),
        ws=np.ascontiguousarray(L1_conv_mag_s_w).reshape(C0, C0 * 9), ws_b=col(L1_conv_mag_s_b),
        wf_in=np.ascontiguousarray(L1_conv_mag_f_w), wf_b=col(L1_conv_mag_f_b),
        ww_t=turned(L1_conv_mag_w), ww_b=row(L1_conv_mag_b), wp_t=turned(L1_conv_pha_w), wp_b=row(L1_conv_pha_b),
        w0_t=turned(L1_conv_conv_0_w), w0_b=row(L1_conv_conv_0_b),
        wc_t=turned(L1_conv_conv_1_w), wc_b=row(L1_conv_conv_1_b), w2_t=turned(L1_conv_conv2_w))
    nc = bacc.Bacc("TRN2", target_bir_lowering=False, num_devices=1)
    nc.disable_value_cache = True
    aps = {k: nc.dram_tensor(k, a.shape, mybir.dt.float32, kind="ExternalInput").ap() for k, a in arrays.items()}
    out = nc.dram_tensor("out", arrays["x"].shape, mybir.dt.float32, kind="ExternalOutput").ap()
    build(nc, at=at, out=out, **aps)
    return run_bass_kernel_spmd(nc, [arrays], core_ids=[0]).results[0]["out"]
```

```python
import math
from contextlib import ExitStack

import numpy as np
import concourse.bass as bass
from concourse import mybir

N, C, H, W = 16, 192, 128, 128
G, CG = 32, 6
Q = 4
LOADS = 4
GQ, CQ = G // Q, C // Q
C1, C0 = C // 4, C // 12
HALF = C // 2
KW = W // 2 + 1
LO = (H - int(H * math.cos(math.pi / 4))) // 2
BOX = int(H * math.cos(math.pi / 4))
WB = 8
WO = WB - 2
NBOX = BOX // WO
T = 2 * (C1 + 1)
EPS = 1e-5
ROUND = 12582912.0
TWO_PI = 6.283185
assert BOX % WO == 0


def frft_matrices():
    n_ = W

    def fftconv(a, kern):
        length = a.shape[-1] + kern.shape[0] - 1
        return np.fft.ifft(np.fft.fft(a, n=length, axis=-1) * np.fft.fft(kern, n=length), axis=-1)

    def chirp(f, a):
        alpha = a * math.pi / 2
        tana2, sina = math.tan(alpha / 2), math.sin(alpha)
        y = np.zeros(f.shape[:-1] + (2 * n_ - 1,), np.complex128)
        y[..., ::2] = f
        fi = fftconv(y, np.sinc(np.arange(-(2 * n_ - 3), 2 * n_ - 2) / 2.0))[..., 2 * n_ - 3:4 * n_ - 4]
        pad = np.zeros(f.shape[:-1] + (n_ - 1,), np.complex128)
        n = np.arange(-2 * n_ + 2, 2 * n_ - 1).astype(np.float64)
        chrp = np.exp(-1j * math.pi / n_ * tana2 / 4 * n ** 2)
        c = math.pi / n_ / sina / 4
        m = np.arange(-(4 * n_ - 4), 4 * n_ - 3).astype(np.float64)
        ret = fftconv(chrp * np.concatenate([pad, fi, pad], axis=-1), np.exp(1j * c * m ** 2))
        ret = chrp * (ret[..., 4 * n_ - 4:8 * n_ - 7] * math.sqrt(c / math.pi))
        return np.exp(-1j * (1 - a) * math.pi / 4) * ret[..., n_ - 1:3 * n_ - 2:2]

    eye = np.eye(n_, dtype=np.complex128)
    forward = chirp(eye, 0.5)
    shift = (np.arange(n_) + n_ // 2) % n_
    centred = (np.fft.ifft(eye[..., shift], axis=-1) * math.sqrt(n_))[..., np.argsort(shift)]
    return forward, chirp(centred, 0.5)


def triple(m):
    return np.concatenate([-m.imag, m.real, m.imag], 1)


def constant_tables():
    fwd, inv = frft_matrices()
    j = np.arange(128)
    turn = np.outer(j, j) % 128
    cos, sin = np.cos(2 * np.pi * turn / 128), np.sin(2 * np.pi * turn / 128)
    cos[turn % 64 == 32] = 0
    sin[turn % 64 == 0] = 0
    dft = cos - 1j * sin
    wgt = np.full(KW, 2.0)
    wgt[[0, KW - 1]] = 1.0
    tab = {}
    tab["frft"] = triple(fwd)
    tab["ifrft"] = triple(inv)
    tab["dft_h"] = np.concatenate([dft.real, dft.imag], 1)
    tab["dft_w"] = triple(dft[:, :KW])
    tab["idft_h"] = triple(np.conj(dft) / H)
    top = np.zeros((128, 128))
    top[:KW] = cos[:KW] * wgt[:, None] / W
    tab["idft_w_re"] = top
    top = np.zeros((128, 128))
    top[:KW] = -sin[:KW] * wgt[:, None] / W
    tab["idft_w_im"] = top
    tab["ident"] = np.eye(128)
    tab["average"] = np.full((128, 128), 1.0 / 128)
    rows = np.zeros((128, 2))
    rows[LO:LO + BOX, 0] = 1
    rows[:, 1] = 1 - rows[:, 0]
    tab["rows"] = rows
    edge = np.ones((128, 2))
    edge[:C0, 0] = 0
    edge[(WB - 1) * C0:, 1] = 0
    tab["edge"] = edge
    lane12 = np.zeros((128, 2 * CG))
    lane12[[C1, 2 * C1 + 1]] = np.tile(np.eye(2), (1, CG))
    tab["lane12"] = lane12
    keep = np.ones((128, 1))
    keep[[C1, 2 * C1 + 1]] = 0
    tab["keep"] = keep
    member = np.zeros((128, 2, G))
    for c in range(HALF):
        for h in range(2):
            member[c, h, (h * HALF + c) // CG] = 1
    tab["member"] = member.reshape(128, 2 * G)
    once = {}
    for k in range(3):
        once[f"band{k}"] = np.eye(128, k=1 - k)
    once["lane"] = np.kron(np.eye(WB), np.ones((C0, 1)))
    for k in range(3):
        once[f"tap{k}"] = np.kron(np.eye(WB, WO, k=-k), np.ones((C0, 1)))
    spread = np.zeros((128, 128))
    spread[:C0] = np.kron(np.ones((1, WB)), np.eye(C0))
    once["spread"] = spread
    spread = np.zeros((128, 128))
    spread[:C1, :T] = np.kron(np.ones((1, 2)), np.eye(C1, C1 + 1))
    once["spread2"] = spread
    lane2 = np.zeros((128, 2))
    lane2[:T] = np.kron(np.eye(2), np.ones((C1 + 1, 1)))
    once["lane2"] = lane2
    at, packed = {}, []
    for tables in (tab, once):
        start = 0
        for name, t in tables.items():
            at[name] = (start, t.shape[1], tables is once)
            start += t.shape[1]
        packed.append(np.concatenate(list(tables.values()), 1).astype(np.float32))
    return packed[0], packed[1], at


def build(nc, x, tables, once, at, l0_w, l0_b, w1, w1_t, ws, ws_b, wf_in, wf_b, ww_t, ww_b,
          wp_t, wp_b, w0_t, w0_b, wc_t, wc_b, w2_t, out):
    f32 = mybir.dt.float32
    ALU = mybir.AluOpType
    ACT = mybir.ActivationFunctionType
    AX = mybir.AxisListType
    ctx = ExitStack()
    with ctx:
        def sb(name, shape):
            return ctx.enter_context(nc.sbuf_tensor(name, shape, f32))

        def sem(name):
            return ctx.enter_context(nc.semaphore(name))

        image = sb("image", [128, C, W])
        mix = sb("mix", [128, W, C1 + 1])
        work_r = sb("work_r", [128, 4, C0 * W])
        FT = len(range(0, KW, WB)) * 128
        work_f = sb("work_f", [128, 2 * FT + 2 * C0 * KW])
        boxed = sb("boxed", [128, NBOX, H + 2])
        hop = sb("hop", [128, 4, 512])
        table = sb("table", [128, sum(k for _, k, o in at.values() if not o)])
        once_sb = work_r[:, 0, 0:sum(k for _, k, o in at.values() if o)]
        ps = ctx.enter_context(nc.psum_tensor("ps", [128, 8, 512], f32))

        def tab(name, rows=128):
            s, k, o = at[name]
            return once_sb[0:rows, s:s + k] if o else table[0:rows, s:s + k]

        def real_row(name):
            k = at[name][1] // 3
            return tab(name)[:, k:3 * k]

        def imag_row(name):
            k = at[name][1] // 3
            return tab(name)[:, 0:2 * k]

        wraw0 = sb("wraw0", [128, 10])
        band = sb("band", [128, 3, 128])
        w1t_sb = sb("w1t_sb", [HALF, 2, C1])
        w1s = sb("w1s", [HALF, 2, C1])
        blk_s = sb("blk_s", [128, 3, C0 * WO])
        blk_f = sb("blk_f", [128, C0 * WB])
        blk_p = sb("blk_p", [128, C0 * WB])
        blk_c = sb("blk_c", [128, C0 * WB])
        blk_o = sb("blk_o", [128, C, 2])
        bias_s = sb("bias_s", [128, C0])
        bias_f = sb("bias_f", [128, C0])
        bias_in = sb("bias_in", [128, C0])
        bias_p = sb("bias_p", [128, C0])
        bias_c = sb("bias_c", [128, C0])
        bias_q = sb("bias_q", [128, C0])
        bias_0 = sb("bias_0", [128, C1])
        bias_1 = sb("bias_1", [128, C1])
        eps_t = sb("eps_t", [128, 1])
        half_pi = sb("half_pi", [128, 1])
        parts = sb("parts", [128, GQ, 12])
        xmv = sb("xmv", [128, 2, GQ, 2])
        ymv = sb("ymv", [128, G, 2])
        dev = sb("dev", [128, G])
        mean0 = sb("mean0", [128, G])
        nmean0 = sb("nmean0", [128, G])
        rstd0 = sb("rstd0", [128, G])
        mean1 = sb("mean1", [128, G])
        rstd1 = sb("rstd1", [128, G])
        tiny = sb("tiny", [128, G])
        prod = sb("prod", [HALF, 2, 2, G])
        col1 = sb("col1", [HALF, 2, 2])
        mrep = hop[0:HALF, 0, 0:2 * 128].rearrange("p (s h) -> p s h", s=2)
        const_o = hop[:, 1, 0:2 * C].rearrange("p (c w) -> p c w", w=2)
        yparts = sb("yparts", [128, GQ, 12])
        scratch = sb("scratch", [128, 1])
        newt = sb("newt", [128, G])

        raw = work_r[:, 3, :]
        off = [0]

        def take(rows, cols):
            s = off[0]
            off[0] += cols
            return raw[0:rows, s:s + cols]

        r_ws = take(C0, C0 * 9)
        r_wf = take(C0, C0)
        r_ww = take(C0, C0)
        r_wp = take(C0, C0)
        r_w0 = take(C0, C0)
        r_wc = take(C0, C0)
        r_w1 = take(C0, C)
        r_w2 = take(C1, C)
        r_bs = take(C0, 1)
        r_bf = take(C0, 1)
        r_bw = take(128, C0)
        r_bp = take(128, C0)
        r_bc = take(128, C0)
        r_b0 = take(128, C0)
        r_bsr = take(C0, 128)
        r_bfr = take(C0, 128)
        r_sp = take(C0, C0 * 9)
        r_fp = take(C0, C0)
        s_exp = work_r[:, 2, 0:C0 * 9]
        f_exp = work_r[:, 2, 256:256 + C0]
        p_exp = work_r[:, 2, 272:272 + C0]
        c_exp = work_r[:, 2, 288:288 + C0]
        s_tmp = work_r[:, 2, 512:512 + C0 * WO]

        S = {k: sem(k) for k in (
            "weights_in", "setup_dve", "setup_pe", "ones_set",
            "x_parts", "x_mean", "x_dev", "x_var", "x_sd", "x_rstd", "centred", "conv", "y_out",
            "y_parts", "y_mean", "y_dev", "y_var", "y_sd", "mix_w", "mix_bias", "mix_ready",
            "y_turned", "turned_a", "turned_b", "mixed", "mix_out",
            "plane_1", "plane_1_out", "plane_2", "plane_2_out",
            "squares", "square_sum", "magnitude", "inverse", "tangent", "arctan", "sign", "fold", "flip", "phase",
            "turned", "turned_out", "box_turned", "box_turned_out", "mag_mixed", "mixed_out",
            "box_mixed", "box_mixed_out", "whole", "fraction", "sine", "z_im", "z_re",
            "back_1", "back_1_out", "back_2", "back_squares", "back_copied",
            "abs_sum", "abs_done", "t_turned", "t_turned_act", "t_turned_dve", "final", "final_out", "link")}
        loaded = [sem(f"loaded{q}") for q in range(Q)]
        stored = [sem(f"stored{q}") for q in range(Q)]

        x_v = x.rearrange("n c h w -> n h c w")
        out_v = out.rearrange("n c h w -> n h c w")
        NW = 26

        def chunk(q):
            return slice(q * CQ, (q + 1) * CQ)

        def parts_of(q):
            step = CQ // LOADS
            return [slice(q * CQ + i * step, q * CQ + (i + 1) * step) for i in range(LOADS)]

        def group(g):
            return slice(g * CG, (g + 1) * CG)

        PAIRS = C0 // 2
        FIRST, COLS = (C0, 2 * C0), (W, KW)

        def buf(k, i):
            if k == 0:
                return work_r[:, i, :]
            s = i * FT if i < 2 else 2 * FT + (i - 2) * C0 * KW
            return work_f[:, s:s + C0 * KW]

        def planes_of(k, i):
            return buf(k, i)[:, 0:C0 * COLS[k]].rearrange("p (w c) -> p c w", c=C0)

        def re_im(k):
            both = work_r[:, 0:2, :] if k == 0 else work_f[:, 0:2 * FT].rearrange("p (r x) -> p r x", r=2)
            return both[:, :, 0:C0 * COLS[k]].rearrange("p r (w c) -> p r c w", c=C0)

        SLICES = [(0, 0, 32), (0, 32, 64), (0, 64, 96), (0, 96, 128), (1, 0, 32), (1, 32, KW)]
        NS = len(SLICES)

        def sl(j, i):
            k, a, b = SLICES[j]
            return buf(k, i)[:, C0 * a:C0 * b]

        UNITS = [(0, 32 * t, 4) for t in range(4)] + [(1, 0, 4), (1, 32, 4), (1, KW - WB, 1)]
        UNIT_SLICE = (0, 1, 2, 3, 4, 5, 5)
        NU = len(UNITS)

        def turned_at(j, m):
            k, a, blocks = UNITS[j]
            s = (a // WB if blocks == 4 else 8) * 128
            if k == 0:
                return work_r[:, m, s:s + blocks * 128]
            return work_f[:, m * FT + s:m * FT + s + blocks * 128]

        FINAL = [(0, CQ, 8), (CQ, CQ, 8), (2 * CQ, 2 * CQ, 4)]
        FINAL_UNITS = [(c, m, w, v) for c, m, w in FINAL for v in range(W // (2 * w))]
        NF = len(FINAL_UNITS)
        READY = (8, 16, 32, 32)

        block = ctx.enter_context(nc.Block())

        @block.sync
        def _(sp):
            for dst, src in ((table[:], tables[:]), (once_sb, once[:]), (wraw0[:, 0:9], l0_w.broadcast_to([128, 9])), (wraw0[:, 9:10], l0_b.broadcast_to([128, 1])),
                             (w1t_sb[:], w1_t.rearrange("(s c) o -> c s o", s=2)),
                             (r_ws, ws), (r_wf, wf_in), (r_ww, ww_t), (r_wp, wp_t), (r_w0, w0_t), (r_wc, wc_t),
                             (r_w1, w1[0:C0, :]), (r_w2, w2_t), (r_bs, ws_b), (r_bf, wf_b),
                             (r_bw, ww_b.broadcast_to([128, C0])), (r_bp, wp_b.broadcast_to([128, C0])), (r_bc, wc_b.broadcast_to([128, C0])), (r_b0, w0_b.broadcast_to([128, C0]))):
                sp.dma_start(dst, src).then_inc(S["weights_in"], 16)
            for q in range(Q):
                for c in parts_of(q):
                    sp.dma_start(image[:, c, :], x_v[0, :, c, :]).then_inc(loaded[q], 16)
            with sp.Fori(0, N - 1) as n:
                for q0, qs in ((0, (0,)), (1, (1,)), (2, (2, 3))):
                    sp.wait_ge(S["final_out"], n * NF + READY[q0])
                    for q in qs:
                        sp.dma_start(out_v[n, :, chunk(q), :], image[:, chunk(q), :]).then_inc(stored[q], 16)
                    for q in qs:
                        sp.wait_ge(stored[q], n * 16 + 16)
                        for c in parts_of(q):
                            sp.dma_start(image[:, c, :], x_v[n + 1, :, c, :]).then_inc(loaded[q], 16)
            for q in range(Q):
                sp.wait_ge(S["final_out"], (N - 1) * NF + READY[q])
                sp.dma_start(out_v[N - 1, :, chunk(q), :], image[:, chunk(q), :]).then_inc(stored[q], 16)
            for q in range(Q):
                sp.wait_ge(stored[q], N * 16)

        @block.tensor
        def _(pe):
            mm, turn = nc.tensor.matmul, nc.tensor.transpose
            ident = tab("ident")
            pe.wait_ge(S["setup_dve"], 1)
            for half in range(2):
                mm(ps[0:HALF, 0, half * C0:(half + 1) * C0], r_w1[:, half * HALF:(half + 1) * HALF], r_w0,
                   start=half == 0, stop=True, skip_group_check=True)
            for t in range(9):
                mm(ps[0:C0, 1, t * C0:(t + 1) * C0], r_ws.rearrange("o (c t) -> o t c", t=9)[:, t, :], r_ww,
                   start=t == 0, stop=True, skip_group_check=True)
            mm(ps[0:C0, 2, 0:C0], r_wf, r_ww, start=True, stop=True)
            mm(ps[:, 3, 0:C0], r_bsr, r_ww, start=True, stop=True)
            mm(ps[:, 4, 0:C0], r_bfr, r_ww, start=True, stop=True)
            mm(ps[0:T, 5, 0:C], tab("spread2", C1)[:, 0:T], r_w2, start=True, stop=True)
            mm(ps[:, 6, 0:C0], tab("spread", C0), r_wp, start=True, stop=True)
            mm(ps[:, 7, 0:C0], tab("spread", C0), r_wc, start=True, stop=True).then_inc(S["setup_pe"], 1)
            pe.wait_ge(S["setup_dve"], 2)
            mm(ps[:, 0, 0:C0 * 9], tab("spread", C0), r_sp, start=True, stop=True)
            mm(ps[:, 1, 0:C0], tab("spread", C0), r_fp, start=True, stop=True).then_inc(S["setup_pe"], 1)
            pe.wait_ge(S["setup_dve"], 3)

            def x_average(n, q):
                pe.wait_ge(S["x_parts"], n * Q + q + 1)
                mm(ps[:, 4, 0:GQ], tab("average"), xmv[:, q % 2, :, 0], start=True, stop=True)\
                    .then_inc(S["x_mean"], 1)

            def x_variance(n, q):
                pe.wait_ge(S["x_dev"], n * Q + q + 1)
                mm(ps[:, 5, 0:GQ], tab("average"), dev[:, 0:GQ], start=True, stop=True)\
                    .then_inc(S["x_var"], 1)

            def conv(n, g):
                pe.wait_ge(S["centred"], n * G + g + 1)
                if g >= 2:
                    pe.wait_ge(S["y_out"], n * G + g - 1)
                for j in range(2):
                    c = slice(g * CG + 3 * j, g * CG + 3 * j + 3)
                    o = ps[:, 2 * (g % 2) + j, 0:3 * W].rearrange("p (c w) -> p c w", c=3)
                    mm(o, band[:, 1, :], image[:, c, :], start=True, stop=False)
                    mm(o[:, :, 1:W], band[:, 0, :], image[:, c, 0:W - 1], start=False, stop=False)
                    last = mm(o[:, :, 0:W - 1], band[:, 2, :], image[:, c, 1:W], start=False, stop=True)
                last.then_inc(S["conv"], 1)

            with pe.Fori(0, N) as n:
                x_average(n, 0)
                x_variance(n, 0)
                for q in range(Q):
                    for g in range(GQ):
                        conv(n, q * GQ + g)
                        if q + 1 < Q and g == 1:
                            x_average(n, q + 1)
                        if q + 1 < Q and g == 4:
                            x_variance(n, q + 1)
                pe.wait_ge(S["y_parts"], n + 1)
                mm(ps[:, 4, 0:G], tab("average"), ymv[:, :, 0], start=True, stop=True).then_inc(S["y_mean"], 1)
                pe.wait_ge(S["y_dev"], n + 1)
                mm(ps[:, 5, 0:G], tab("average"), dev[:], start=True, stop=True).then_inc(S["y_var"], 1)
                pe.wait_ge(S["mix_w"], n + 1)
                for half in range(2):
                    last = mm(ps[:, 6, 0:C1], mrep[:, half, :], w1s[:, half, :], start=half == 0, stop=half == 1)
                last.then_inc(S["mix_bias"], 1)
                pe.wait_ge(S["mix_ready"], n + 1)

                def mix_block(b):
                    pe.wait_ge(S["turned_a"], n * 32 + b + 1)
                    pe.wait_ge(S["turned_b"], n * 32 + b + 1)
                    if b % 2 == 0 and b >= 4:
                        pe.wait_ge(S["mix_out"], n * 16 + b // 2 - 1)
                    for i in range(4):
                        o = ps[:, (b // 2) % 2, ((b % 2) * 4 + i) * C1:((b % 2) * 4 + i + 1) * C1]
                        for half in range(2):
                            last = mm(o, work_r[0:HALF, b % 4, (4 * half + i) * 128:(4 * half + i + 1) * 128],
                                      w1s[:, half, :], start=half == 0, stop=half == 1)
                    last.then_inc(S["mixed"], 1)

                for b in range(32):
                    if b >= 3:
                        pe.wait_ge(S["turned_a"], n * 32 + b - 2)
                        pe.wait_ge(S["turned_b"], n * 32 + b - 2)
                    for half in range(2):
                        for i in range(4):
                            last = turn(ps[0:HALF, 2 + 2 * (b % 3) + half, i * 128:(i + 1) * 128],
                                        image[:, half * HALF:(half + 1) * HALF, 4 * b + i], ident)
                    last.then_inc(S["y_turned"], 1)
                    if b >= 2:
                        mix_block(b - 2)
                mix_block(30)
                mix_block(31)
                pe.wait_ge(S["mix_out"], n * 16 + 16)

                def plane_1(u):
                    k, p = divmod(u, PAIRS)
                    if u >= 2:
                        pe.wait_ge(S["plane_1_out"], n * 2 * PAIRS + u - 1)
                    for i in range(2):
                        last = mm(ps[:, u % 2, i * 256:(i + 1) * 256], mix[:, :, FIRST[k] + 2 * p + i],
                                  tab("dft_h") if k else real_row("frft"), start=True, stop=True)
                    last.then_inc(S["plane_1"], 1)

                def plane_2(u):
                    k, cols = u // PAIRS, COLS[u // PAIRS]
                    name = "dft_w" if k else "frft"
                    pe.wait_ge(S["plane_1_out"], n * 2 * PAIRS + u + 1)
                    if u >= 2:
                        pe.wait_ge(S["plane_2_out"], n * 2 * PAIRS + u - 1)
                    for i in range(2):
                        o = ps[:, 2 + u % 2, i * 2 * cols:(i + 1) * 2 * cols]
                        a = hop[:, u % 2, i * 256:(i + 1) * 256]
                        mm(o, a[:, 0:128], real_row(name), start=True, stop=False)
                        last = mm(o, a[:, 128:256], imag_row(name), start=False, stop=True)
                    last.then_inc(S["plane_2"], 1)

                for u in range(2 * PAIRS):
                    plane_1(u)
                    if u >= 1:
                        plane_2(u - 1)
                plane_2(2 * PAIRS - 1)
                pe.wait_ge(S["plane_2_out"], n * 2 * PAIRS + 2 * PAIRS)

                def turn_unit(j):
                    k, a, blocks = UNITS[j]
                    pe.wait_ge(S["phase"], n * NS + UNIT_SLICE[j] + 1)
                    if j >= 1:
                        pe.wait_ge(S["turned_out"], n * NU + j)
                    for m in range(2):
                        for i in range(blocks):
                            c = C0 * (a + WB * i)
                            last = turn(ps[:, 4 + m, i * 128:(i + 1) * 128], buf(k, 2 + m)[:, c:c + C0 * WB], ident)
                    last.then_inc(S["turned"], 1)

                def mix_unit(j):
                    k, a, blocks = UNITS[j]
                    pe.wait_ge(S["turned_out"], n * NU + j + 1)
                    if j >= 1:
                        pe.wait_ge(S["mixed_out"], n * NU + j)
                    for m, weights in enumerate((blk_c, blk_c) if k else (blk_f, blk_p)):
                        for i in range(blocks):
                            last = mm(ps[:, 6 + m, i * 128:(i + 1) * 128],
                                      turned_at(j, m)[:, i * 128:(i + 1) * 128], weights[:], start=True, stop=True)
                    last.then_inc(S["mag_mixed"], 1)

                def turn_box(t):
                    if t >= 2:
                        pe.wait_ge(S["box_turned_out"], n * 4 + t - 1)
                    for i, j in enumerate(range(4 * t, min(4 * t + 4, NBOX))):
                        c = C0 * (LO - 1 + WO * j)
                        last = turn(ps[:, t % 2, i * 128:(i + 1) * 128], work_r[:, 2, c:c + C0 * WB], ident)
                    last.then_inc(S["box_turned"], 1)

                def conv_box(t):
                    for i in range(5):
                        o = ps[:, 1 + t, i * C0 * WO:(i + 1) * C0 * WO]
                        for dy in range(3):
                            last = mm(o, boxed[:, 5 * t + i, dy:dy + 128], blk_s[:, dy, :],
                                      start=dy == 0, stop=dy == 2)
                    last.then_inc(S["box_mixed"], 1)

                turn_unit(0)
                turn_unit(1)
                turn_box(0)
                mix_unit(0)
                turn_unit(2)
                turn_box(1)
                turn_box(2)
                mix_unit(1)
                turn_unit(3)
                turn_box(3)
                mix_unit(2)
                turn_unit(4)
                mix_unit(3)
                pe.wait_ge(S["box_turned_out"], n * 4 + 4)
                for t in range(3):
                    conv_box(t)
                turn_unit(5)
                mix_unit(4)
                turn_unit(6)
                mix_unit(5)
                mix_unit(6)

                def back_1(u):
                    k, p = divmod(u, PAIRS)
                    cols, name = COLS[k], "idft_h" if k else "ifrft"
                    if u == 0:
                        pe.wait_ge(S["z_re"], n * NS + 4)
                        pe.wait_ge(S["z_im"], n * NS + 4)
                    if u == PAIRS:
                        pe.wait_ge(S["z_re"], n * NS + NS)
                        pe.wait_ge(S["z_im"], n * NS + NS)
                    if u >= 2:
                        pe.wait_ge(S["back_1_out"], n * 2 * PAIRS + u - 1)
                    for i in range(2):
                        o = ps[0:cols, u % 2, i * 256:(i + 1) * 256]
                        mm(o, planes_of(k, 0)[:, 2 * p + i, :], real_row(name), start=True, stop=False)
                        last = mm(o, planes_of(k, 1)[:, 2 * p + i, :], imag_row(name), start=False, stop=True)
                    last.then_inc(S["back_1"], 1)

                def back_2(u):
                    k, cols = u // PAIRS, COLS[u // PAIRS]
                    pe.wait_ge(S["back_1_out"], n * 2 * PAIRS + u + 1)
                    if u >= 2 and u - 2 < PAIRS:
                        pe.wait_ge(S["back_squares"], n * PAIRS + u - 1)
                    elif u >= 2:
                        pe.wait_ge(S["back_copied"], n * PAIRS + u - 1 - PAIRS)
                    re, im = (tab("idft_w_re", KW), tab("idft_w_im", KW)) if k else (real_row("ifrft"), imag_row("ifrft"))
                    wide = 128 if k else 256
                    for i in range(2):
                        a = hop[0:cols, u % 2, i * 256:(i + 1) * 256]
                        o = ps[:, 2 + u % 2, i * wide:(i + 1) * wide]
                        mm(o, a[:, 0:128], re, start=True, stop=False)
                        last = mm(o, a[:, 128:256], im, start=False, stop=True)
                    last.then_inc(S["back_2"], 1)

                for u in range(2 * PAIRS):
                    back_1(u)
                    if u >= 1:
                        back_2(u - 1)
                back_2(2 * PAIRS - 1)
                pe.wait_ge(S["back_copied"], n * PAIRS + PAIRS)

                pe.wait_ge(S["abs_done"], n + 1)
                for t in range(16):
                    if t >= 4:
                        pe.wait_ge(S["t_turned_act" if t % 2 == 0 else "t_turned_dve"], n * 8 + t // 2 - 1)
                    for i in range(4):
                        j = 4 * t + i
                        last = turn(ps[0:T, t % 4, i * 128:(i + 1) * 128], mix[:, 2 * j:2 * j + 2, :], ident)
                    last.then_inc(S["t_turned"], 1)
                pe.wait_ge(S["t_turned_act"], n * 8 + 8)
                pe.wait_ge(S["t_turned_dve"], n * 8 + 8)
                turned = work_r[:].rearrange("p a (b h) -> p (a b) h", h=128)
                for u, (c, m, w, v) in enumerate(FINAL_UNITS):
                    if u >= 4:
                        pe.wait_ge(S["final_out"], n * NF + u - 3)
                    for bank in range(2):
                        o = ps[:, 2 * (u % 4) + bank, 0:w * m].rearrange("p (c w) -> p c w", w=w)
                        for i in range(w // 2):
                            last = mm(o[:, :, 2 * i:2 * i + 2], turned[0:T, (2 * v + bank) * (w // 2) + i, :],
                                      blk_o[0:T, c:c + m, :], start=i == 0, stop=True, skip_group_check=True)
                    last.then_inc(S["final"], 1)

        @block.scalar
        def _(act):
            act.wait_ge(S["setup_dve"], 3)
            with act.Fori(0, N) as n:
                def centre(g):
                    nc.scalar.activation(image[:, group(g), :], image[:, group(g), :], ACT.Identity,
                                         bias=nmean0[:, g:g + 1]).then_inc(S["centred"], 1)

                def x_sd(q):
                    act.wait_ge(S["x_var"], n * Q + q + 1)
                    nc.scalar.activation(tiny[:, 0:GQ], ps[:, 5, 0:GQ], ACT.Sqrt, bias=eps_t[:]).then_inc(S["x_sd"], 1)

                x_sd(0)
                for q in range(Q):
                    act.wait_ge(S["x_rstd"], n * Q + q + 1)
                    for g in range(GQ):
                        centre(q * GQ + g)
                    if q + 1 < Q:
                        x_sd(q + 1)
                act.wait_ge(S["y_var"], n + 1)
                nc.scalar.activation(tiny[:], ps[:, 5, 0:G], ACT.Sqrt, bias=eps_t[:]).then_inc(S["y_sd"], 1)
                for b in range(32):
                    act.wait_ge(S["y_turned"], n * 32 + b + 1)
                    if b >= 4:
                        act.wait_ge(S["mixed"], n * 32 + b - 3)
                    nc.scalar.copy(work_r[0:HALF, b % 4, 0:512], ps[0:HALF, 2 + 2 * (b % 3), :]).then_inc(S["turned_a"], 1)
                act.wait_ge(S["mixed"], n * 32 + 32)

                pa = n * 2 * PAIRS

                def plane_1_out(u):
                    act.wait_ge(S["plane_1"], pa + u + 1)
                    if u >= 2:
                        act.wait_ge(S["plane_2"], pa + u - 1)
                    nc.scalar.copy(hop[:, u % 2, :], ps[:, u % 2, :]).then_inc(S["plane_1_out"], 1)

                def plane_2_out(u):
                    p = u - PAIRS
                    act.wait_ge(S["plane_2"], pa + u + 1)
                    nc.scalar.copy(re_im(1)[:, :, 2 * p:2 * p + 2, :],
                                   ps[:, 2 + u % 2, 0:4 * KW].rearrange("p (c r w) -> p r c w", c=2, r=2))\
                        .then_inc(S["plane_2_out"], 1)

                def fourier_out(i):
                    if i < PAIRS:
                        plane_1_out(PAIRS + i)
                    if i >= 1:
                        plane_2_out(PAIRS + i - 1)

                def squares(j):
                    if j == 0:
                        act.wait_ge(S["plane_2_out"], pa + PAIRS)
                    if j == 4:
                        act.wait_ge(S["plane_2_out"], pa + 2 * PAIRS)
                    nc.scalar.activation(sl(j, 2), sl(j, 0), ACT.Square)
                    nc.scalar.activation(sl(j, 3), sl(j, 1), ACT.Square).then_inc(S["squares"], 1)

                def magnitude(j):
                    act.wait_ge(S["square_sum"], n * NS + j + 1)
                    nc.scalar.activation(sl(j, 2), sl(j, 2), ACT.Sqrt)
                    nc.scalar.activation(sl(j, 3), sl(j, 0), ACT.Abs).then_inc(S["magnitude"], 1)

                def arctan(j):
                    act.wait_ge(S["tangent"], n * NS + j + 1)
                    nc.scalar.activation(sl(j, 3), sl(j, 3), ACT.Arctan).then_inc(S["arctan"], 1)

                def turned_out(j):
                    blocks = UNITS[j][2]
                    act.wait_ge(S["turned"], n * NU + j + 1)
                    nc.scalar.copy(turned_at(j, 0), ps[:, 4, 0:blocks * 128])
                    nc.scalar.mul(turned_at(j, 1), ps[:, 5, 0:blocks * 128], 2 / math.pi).then_inc(S["turned_out"], 1)

                def sine(j):
                    act.wait_ge(S["fraction"], n * NS + j + 1)
                    nc.scalar.activation(sl(j, 1), sl(j, 0), ACT.Sin, scale=TWO_PI)
                    nc.scalar.activation(sl(j, 3), sl(j, 0), ACT.Abs).then_inc(S["sine"], 1)
                    act.wait_ge(S["sine"], (n * NS + j) * 2 + 1)
                    nc.scalar.activation(sl(j, 3), sl(j, 3), ACT.Sin, scale=-TWO_PI, bias=half_pi[:]).then_inc(S["sine"], 1)

                for u in range(PAIRS):
                    plane_1_out(u)
                squares(0)
                fourier_out(0)
                squares(1)
                fourier_out(1)
                magnitude(0)
                fourier_out(2)
                squares(2)
                fourier_out(3)
                magnitude(1)
                fourier_out(4)
                squares(3)
                fourier_out(5)
                magnitude(2)
                fourier_out(6)
                magnitude(3)
                fourier_out(7)
                fourier_out(8)
                arctan(0)
                arctan(1)
                turned_out(0)
                arctan(2)
                turned_out(1)
                arctan(3)
                squares(4)
                squares(5)
                turned_out(2)
                magnitude(4)
                magnitude(5)
                turned_out(3)
                arctan(4)
                arctan(5)
                turned_out(4)
                sine(0)
                sine(1)
                turned_out(5)
                sine(2)
                sine(3)
                turned_out(6)
                sine(4)
                sine(5)

                def back_1_out(u):
                    cols = COLS[u // PAIRS]
                    act.wait_ge(S["back_1"], pa + u + 1)
                    if u >= 2:
                        act.wait_ge(S["back_2"], pa + u - 1)
                    nc.scalar.copy(hop[0:cols, u % 2, :], ps[0:cols, u % 2, :]).then_inc(S["back_1_out"], 1)

                def back_squares(u):
                    act.wait_ge(S["back_2"], pa + u + 1)
                    if u >= 2:
                        act.wait_ge(S["abs_sum"], n * PAIRS + u - 1)
                    nc.scalar.activation(hop[:, 2 + u % 2, :], ps[:, 2 + u % 2, :], ACT.Square).then_inc(S["back_squares"], 1)

                for u in range(2 * PAIRS):
                    back_1_out(u)
                    if 1 <= u <= PAIRS:
                        back_squares(u - 1)
                    if u == PAIRS + 2:
                        act.wait_ge(S["abs_sum"], n * PAIRS + PAIRS)
                        nc.scalar.activation(mix[:, :, C0:2 * C0], mix[:, :, C0:2 * C0], ACT.Sqrt).then_inc(S["abs_done"], 1)
                for t in range(0, 16, 2):
                    act.wait_ge(S["t_turned"], n * 16 + t + 1)
                    nc.scalar.copy(work_r[0:T, t // 4, 512 * (t % 4):512 * (t % 4) + 512], ps[0:T, t % 4, :])\
                        .then_inc(S["t_turned_act"], 1)

        @block.gpsimd
        def _(pool):
            pool.memset(mix[:, :, C1:C1 + 1], 1.0).then_inc(S["ones_set"], 1)
            with pool.Fori(0, N) as n:
                def square_sum(j):
                    pool.wait_ge(S["squares"], n * NS + j + 1)
                    nc.gpsimd.tensor_tensor(sl(j, 2), sl(j, 2), sl(j, 3), ALU.add).then_inc(S["square_sum"], 1)

                def tangent(j):
                    pool.wait_ge(S["inverse"], (n * NS + j) * 2 + 2)
                    nc.gpsimd.tensor_tensor(sl(j, 3), sl(j, 1), sl(j, 3), ALU.mult).then_inc(S["tangent"], 1)

                def fraction(j):
                    pool.wait_ge(S["whole"], n * NS + j + 1)
                    nc.gpsimd.tensor_tensor(sl(j, 0), sl(j, 3), sl(j, 0), ALU.subtract).then_inc(S["fraction"], 1)

                def z_im(j):
                    pool.wait_ge(S["sine"], (n * NS + j) * 2 + 2)
                    if j < 4:
                        pool.wait_ge(S["box_mixed_out"], n * 3 + 3)
                    nc.gpsimd.tensor_tensor(sl(j, 1), sl(j, 2), sl(j, 1), ALU.mult).then_inc(S["z_im"], 1)

                for j in range(4):
                    square_sum(j)
                for j in range(4):
                    tangent(j)
                square_sum(4)
                square_sum(5)
                tangent(4)
                tangent(5)
                for j in range(5):
                    fraction(j)
                for j in range(4):
                    z_im(j)
                fraction(5)
                z_im(4)
                z_im(5)
                for u in range(PAIRS):
                    pool.wait_ge(S["back_squares"], n * PAIRS + u + 1)
                    v = hop[:, 2 + u % 2, :].rearrange("p (c r w) -> p c r w", c=2, r=2)
                    nc.gpsimd.tensor_tensor(mix[:, :, C0 + 2 * u:C0 + 2 * u + 2].rearrange("p w c -> p c w"),
                                            v[:, :, 0, :], v[:, :, 1, :], ALU.add).then_inc(S["abs_sum"], 1)

        @block.vector
        def _(dve):
            v = nc.vector
            linked = [0, None, 0]

            def link(ins):
                linked[0] += 1
                ins.then_inc(S["link"], 1)
                value = linked[0]
                if linked[1] is not None:
                    value = linked[1] * LINKS + value
                dve.wait_ge(S["link"], value)

            v.memset(eps_t[:], EPS)
            v.memset(half_pi[:], math.pi / 2)
            v.memset(bias_0[:], 0.0)
            dve.wait_ge(S["weights_in"], 19 * 16)
            v.memset(boxed[:], 0.0)
            v.tensor_scalar(r_bsr, tab("average", C0), r_bs, 128.0, ALU.mult, ALU.mult)
            v.tensor_scalar(r_bfr, tab("average", C0), r_bf, 128.0, ALU.mult, ALU.mult).then_inc(S["setup_dve"], 1)
            for kx in range(3):
                link(v.tensor_scalar(band[:, kx, :], tab("band0"), wraw0[:, kx:kx + 1], None, ALU.mult))
                for ky in (1, 2):
                    link(v.scalar_tensor_tensor(band[:, kx, :], tab(f"band{ky}"), wraw0[:, 3 * ky + kx:3 * ky + kx + 1],
                                                band[:, kx, :], ALU.mult, ALU.add))
            dve.wait_ge(S["setup_pe"], 1)
            v.tensor_copy(w1t_sb[:, :, 0:C0], ps[0:HALF, 0, 0:2 * C0].rearrange("p (s o) -> p s o", s=2))
            v.tensor_copy(r_sp, ps[0:C0, 1, 0:9 * C0])
            v.tensor_copy(r_fp, ps[0:C0, 2, 0:C0])
            v.tensor_tensor(bias_s[:], ps[:, 3, 0:C0], r_bw, ALU.add)
            link(v.tensor_tensor(bias_f[:], ps[:, 4, 0:C0], r_bw, ALU.add))
            link(v.tensor_scalar(bias_in[:], bias_s[:], tab("rows")[:, 0:1], None, ALU.mult))
            v.scalar_tensor_tensor(bias_in[:], bias_f[:], tab("rows")[:, 1:2], bias_in[:], ALU.mult, ALU.add)
            v.tensor_copy(p_exp, ps[:, 6, 0:C0])
            v.tensor_copy(c_exp, ps[:, 7, 0:C0])
            v.tensor_copy(bias_c[:], r_bc)
            v.tensor_copy(bias_0[:, 0:C0], r_b0)
            v.tensor_scalar(bias_p[:], r_bp, 1 / (2 * math.pi), None, ALU.mult)
            v.tensor_scalar(bias_q[:], r_bc, 1 / (2 * math.pi), None, ALU.mult)
            link(v.tensor_tensor(blk_o[0:T], ps[0:T, 5, 0:C].rearrange("p (c w) -> p c w", w=1).broadcast_to([T, C, 2]),
                                 tab("lane2", T).rearrange("p (c w) -> p c w", c=1).broadcast_to([T, C, 2]), ALU.mult))
            v.memset(dev[:, 0:1], 0.0).then_inc(S["setup_dve"], 1)
            dve.wait_ge(S["setup_pe"], 2)
            v.tensor_copy(s_exp, ps[:, 0, 0:9 * C0])
            link(v.tensor_copy(f_exp, ps[:, 1, 0:C0]))

            def spread(dst, src, mask, w):
                return v.tensor_tensor(dst.rearrange("p (b o) -> p b o", b=w),
                                       src.rearrange("p (b o) -> p b o", b=1).broadcast_to([128, w, C0]),
                                       mask.rearrange("p (b o) -> p b o", o=1).broadcast_to([128, w, C0]), ALU.mult)

            link(spread(blk_f[:], f_exp, tab("lane"), WB))
            link(spread(blk_c[:], c_exp, tab("lane"), WB))
            link(spread(blk_p[:], p_exp, tab("lane"), WB))
            for ky in range(3):
                link(spread(blk_s[:, ky, :], s_exp[:, 3 * ky * C0:(3 * ky + 1) * C0], tab("tap0"), WO))
                for kx in (1, 2):
                    link(spread(s_tmp, s_exp[:, (3 * ky + kx) * C0:(3 * ky + kx + 1) * C0], tab(f"tap{kx}"), WO))
                    link(v.tensor_tensor(blk_s[:, ky, :], blk_s[:, ky, :], s_tmp, ALU.add))
            dve.wait_ge(S["ones_set"], 1)
            v.memset(dev[:, 0:1], 0.0).then_inc(S["setup_dve"], 1)

            LINKS = 43
            SETUP_LINKS = linked[0]
            def newton(dst, sd, var, k):
                t = newt[:, 0:k]
                link(v.reciprocal(dst, sd))
                link(v.tensor_tensor(t, dst, dst, ALU.mult))
                link(v.scalar_tensor_tensor(t, var, EPS, t, ALU.add, ALU.mult))
                link(v.tensor_scalar(t, t, -0.5, 1.5, ALU.mult, ALU.add))
                return v.tensor_tensor(dst, dst, t, ALU.mult)

            with dve.Fori(0, N) as n:
                linked[1] = n

                def x_parts(q):
                    dve.wait_ge(loaded[q], n * 16 * LOADS + 16 * LOADS)
                    for g in range(GQ):
                        for j in range(2):
                            c = (q * GQ + g) * CG + 3 * j
                            last = v.bn_stats(parts[:, g, 6 * j:6 * j + 6], image[:, c:c + 3, :])
                    link(last)
                    v.memset(scratch[:], 0.0)
                    for g in range(GQ):
                        last = v.bn_aggr(xmv[:, q % 2, g, :], parts[:, g, :])
                    last.then_inc(S["x_parts"], 1)

                def x_dev(q):
                    gs = slice(q * GQ, (q + 1) * GQ)
                    dve.wait_ge(S["x_mean"], n * Q + q + 1)
                    v.tensor_copy(mean0[:, gs], ps[:, 4, 0:GQ])
                    v.tensor_scalar(nmean0[:, gs], ps[:, 4, 0:GQ], -1.0, None, ALU.mult)
                    link(v.tensor_tensor(dev[:, 0:GQ], xmv[:, q % 2, :, 0], ps[:, 4, 0:GQ], ALU.subtract))
                    link(v.tensor_tensor(dev[:, 0:GQ], dev[:, 0:GQ], dev[:, 0:GQ], ALU.mult))
                    v.tensor_tensor(dev[:, 0:GQ], dev[:, 0:GQ], xmv[:, q % 2, :, 1], ALU.add).then_inc(S["x_dev"], 1)

                def x_rstd(q):
                    gs = slice(q * GQ, (q + 1) * GQ)
                    dve.wait_ge(S["x_sd"], n * Q + q + 1)
                    newton(rstd0[:, gs], tiny[:, 0:GQ], ps[:, 5, 0:GQ], GQ).then_inc(S["x_rstd"], 1)

                x_parts(0)
                x_dev(0)
                x_rstd(0)
                dve.wait_ge(S["x_rstd"], n * Q + 1)
                for q in range(Q):
                    if q + 1 < Q:
                        x_parts(q + 1)
                    for i in range(GQ):
                        g = q * GQ + i
                        dve.wait_ge(S["conv"], n * G + g + 1)
                        o = ps[:, 2 * (g % 2):2 * (g % 2) + 2, 0:3 * W]
                        y = image[:, group(g), :].rearrange("p (a c) w -> p a (c w)", a=2)
                        v.scalar_tensor_tensor(y, o, rstd0[:, g:g + 1], y, ALU.mult, ALU.add).then_inc(S["y_out"], 1)
                        dve.wait_ge(S["y_out"], n * G + g + 1)
                        for j in range(2):
                            last = v.bn_stats(yparts[:, i, 6 * j:6 * j + 6], image[:, g * CG + 3 * j:g * CG + 3 * j + 3, :])
                        if q + 1 < Q and i == 2:
                            x_dev(q + 1)
                        if q + 1 < Q and i == 5:
                            x_rstd(q + 1)
                    link(last)
                    v.memset(scratch[:], 0.0)
                    for i in range(GQ):
                        last = v.bn_aggr(ymv[:, q * GQ + i, :], yparts[:, i, :])
                last.then_inc(S["y_parts"], 1)
                dve.wait_ge(S["y_mean"], n + 1)
                v.tensor_copy(mean1[:], ps[:, 4, 0:G])
                link(v.tensor_tensor(dev[:], ymv[:, :, 0], ps[:, 4, 0:G], ALU.subtract))
                link(v.tensor_tensor(dev[:], dev[:], dev[:], ALU.mult))
                v.tensor_tensor(dev[:], dev[:], ymv[:, :, 1], ALU.add).then_inc(S["y_dev"], 1)
                dve.wait_ge(S["y_sd"], n + 1)
                link(newton(rstd1[:], tiny[:], ps[:, 5, 0:G], G))
                member = tab("member", HALF).rearrange("p (s g) -> p s g", s=2)
                for j, src in enumerate((rstd1, mean1)):
                    last = v.tensor_tensor(prod[:, j], member,
                                           src[0:HALF].rearrange("p (s g) -> p s g", s=1).broadcast_to([HALF, 2, G]), ALU.mult)
                link(last)
                link(v.tensor_reduce(col1[:].rearrange("p a b -> p (a b)"), prod[:].rearrange("p a b g -> p (a b) g"), AX.X, ALU.add))
                for half in range(2):
                    v.tensor_scalar(w1s[:, half, :], w1t_sb[:, half, :], col1[:, 0, half:half + 1], None, ALU.mult)
                    last = v.tensor_scalar(mrep[:, half, :], tab("average", HALF), col1[:, 1, half:half + 1], 128.0,
                                           ALU.mult, ALU.mult)
                last.then_inc(S["mix_w"], 1)
                dve.wait_ge(S["mix_bias"], n + 1)
                v.tensor_tensor(bias_1[:], bias_0[:], ps[:, 6, 0:C1], ALU.subtract)
                link(v.tensor_scalar(tiny[:], mean0[:], wraw0[:, 9:10], None, ALU.add))
                link(v.tensor_tensor(const_o[0:T].rearrange("p (g c) w -> p g (c w)", g=G),
                                     tiny[0:T].rearrange("p (g c) -> p g c", c=1).broadcast_to([T, G, 2 * CG]),
                                     tab("lane12", T).rearrange("p (g c) -> p g c", g=1).broadcast_to([T, G, 2 * CG]),
                                     ALU.mult))
                v.scalar_tensor_tensor(blk_o[0:T], blk_o[0:T], tab("keep", T), const_o[0:T], ALU.mult, ALU.add)\
                    .then_inc(S["mix_ready"], 1)
                dve.wait_ge(S["mix_ready"], n + 1)

                def mix_out(u):
                    dve.wait_ge(S["mixed"], n * 32 + 2 * u + 2)
                    v.tensor_tensor(mix[:, 8 * u:8 * u + 8, 0:C1],
                                    ps[:, u % 2, 0:8 * C1].rearrange("p (w o) -> p w o", w=8),
                                    bias_1[:].rearrange("p (w o) -> p w o", w=1).broadcast_to([128, 8, C1]), ALU.add)\
                        .then_inc(S["mix_out"], 1)

                for b in range(32):
                    dve.wait_ge(S["y_turned"], n * 32 + b + 1)
                    if b >= 4:
                        dve.wait_ge(S["mixed"], n * 32 + b - 3)
                    v.tensor_copy(work_r[0:HALF, b % 4, 512:1024], ps[0:HALF, 3 + 2 * (b % 3), :]).then_inc(S["turned_b"], 1)
                    if b >= 3 and b % 2:
                        mix_out((b - 3) // 2)
                mix_out(15)

                for u in range(PAIRS):
                    dve.wait_ge(S["plane_2"], n * 2 * PAIRS + u + 1)
                    v.tensor_copy(re_im(0)[:, :, 2 * u:2 * u + 2, :],
                                  ps[:, 2 + u % 2, :].rearrange("p (c r w) -> p r c w", c=2, r=2))\
                        .then_inc(S["plane_2_out"], 1)

                def inverse(j):
                    dve.wait_ge(S["magnitude"], n * NS + j + 1)
                    v.scalar_tensor_tensor(sl(j, 3), sl(j, 2), 1e-30, sl(j, 3), ALU.max, ALU.add).then_inc(S["inverse"], 1)
                    dve.wait_ge(S["inverse"], (n * NS + j) * 2 + 1)
                    v.reciprocal(sl(j, 3), sl(j, 3)).then_inc(S["inverse"], 1)

                def phase(j):
                    dve.wait_ge(S["arctan"], n * NS + j + 1)
                    v.tensor_scalar(sl(j, 1), sl(j, 1), 0.0, 0.5, ALU.is_ge, ALU.subtract)
                    v.tensor_scalar(sl(j, 0), sl(j, 0), 0.0, 0.5, ALU.is_ge, ALU.subtract).then_inc(S["sign"], 1)
                    dve.wait_ge(S["sign"], n * NS + j + 1)
                    v.scalar_tensor_tensor(sl(j, 3), sl(j, 1), -math.pi / 2, sl(j, 3), ALU.mult, ALU.add).then_inc(S["fold"], 1)
                    dve.wait_ge(S["fold"], n * NS + j + 1)
                    v.tensor_tensor(sl(j, 3), sl(j, 3), sl(j, 0), ALU.mult).then_inc(S["flip"], 1)
                    dve.wait_ge(S["flip"], n * NS + j + 1)
                    v.scalar_tensor_tensor(sl(j, 3), sl(j, 1), math.pi / 4, sl(j, 3), ALU.mult, ALU.add).then_inc(S["phase"], 1)

                def box_out(t):
                    m = min(4, NBOX - 4 * t)
                    dve.wait_ge(S["box_turned"], n * 4 + t + 1)
                    src = ps[:, t % 2, 0:m * 128].rearrange("p (j h) -> p j h", j=m)[:, :, LO:LO + BOX]
                    dst = boxed[:, 4 * t:4 * t + m, LO + 1:LO + BOX + 1]
                    a, b = (1 if t == 0 else 0), (m - 1 if t == 3 else m)
                    if t == 0:
                        v.tensor_scalar(dst[:, 0, :], src[:, 0, :], tab("edge")[:, 0:1], None, ALU.mult)
                    if t == 3:
                        v.tensor_scalar(dst[:, m - 1, :], src[:, m - 1, :], tab("edge")[:, 1:2], None, ALU.mult)
                    v.tensor_copy(dst[:, a:b, :], src[:, a:b, :]).then_inc(S["box_turned_out"], 1)

                def mixed_out(j):
                    k, a, blocks = UNITS[j]
                    first, end = (KW - 1, KW) if blocks == 1 else (a, a + WB * blocks)
                    dve.wait_ge(S["mag_mixed"], n * NU + j + 1)
                    for m, bias in enumerate((bias_c, bias_q) if k else (bias_f, bias_p)):
                        inner = (max(first, LO), min(end, LO + BOX)) if k == 0 and m == 0 else (end, end)
                        for lo, hi, inside in ((first, inner[0], False), (*inner, True), (max(inner[1], first), end, False)):
                            if lo >= hi or (not inside and (lo, hi) == (end, end)):
                                continue
                            o = buf(k, 2 + m)[:, C0 * lo:C0 * hi].rearrange("p (w o) -> p w o", o=C0)
                            i = ps[:, 6 + m, C0 * (lo - a):C0 * (hi - a)].rearrange("p (w o) -> p w o", o=C0)
                            z = (bias_in if inside else bias)[:].rearrange("p (w o) -> p w o", w=1).broadcast_to([128, hi - lo, C0])
                            if inside:
                                last = v.scalar_tensor_tensor(o, i, tab("rows")[:, 1:2], z, ALU.mult, ALU.add)
                            else:
                                last = v.tensor_tensor(o, i, z, ALU.add)
                    last.then_inc(S["mixed_out"], 1)

                def whole(j):
                    dve.wait_ge(S["mixed_out"], n * NU + (j + 1 if j < 5 else NU))
                    v.tensor_scalar(sl(j, 0), sl(j, 3), ROUND, ROUND, ALU.add, ALU.subtract).then_inc(S["whole"], 1)

                def conv_out(t):
                    dve.wait_ge(S["box_mixed"], n * 3 + t + 1)
                    c = C0 * (LO + 30 * t)
                    o = work_r[:, 2, c:c + 480]
                    v.scalar_tensor_tensor(o, ps[:, 1 + t, 0:480], tab("rows")[:, 0:1], o, ALU.mult, ALU.add)\
                        .then_inc(S["box_mixed_out"], 1)

                def z_re(j):
                    dve.wait_ge(S["sine"], (n * NS + j) * 2 + 2)
                    if j == 0:
                        dve.wait_ge(S["box_mixed_out"], n * 3 + 3)
                    v.tensor_tensor(sl(j, 0), sl(j, 2), sl(j, 3), ALU.mult).then_inc(S["z_re"], 1)

                inverse(0)
                inverse(1)
                phase(0)
                inverse(2)
                phase(1)
                box_out(0)
                inverse(3)
                mixed_out(0)
                phase(2)
                box_out(1)
                box_out(2)
                whole(0)
                mixed_out(1)
                phase(3)
                inverse(4)
                box_out(3)
                whole(1)
                mixed_out(2)
                inverse(5)
                phase(4)
                whole(2)
                mixed_out(3)
                phase(5)
                whole(3)
                for t in range(3):
                    conv_out(t)
                mixed_out(4)
                whole(4)
                for j in range(4):
                    z_re(j)
                mixed_out(5)
                mixed_out(6)
                whole(5)
                z_re(4)
                z_re(5)
                for u in range(PAIRS, 2 * PAIRS):
                    p = u - PAIRS
                    dve.wait_ge(S["back_2"], n * 2 * PAIRS + u + 1)
                    v.tensor_copy(mix[:, :, 2 * C0 + 2 * p:2 * C0 + 2 * p + 2].rearrange("p w c -> p c w"),
                                  ps[:, 2 + u % 2, 0:256].rearrange("p (c w) -> p c w", c=2)).then_inc(S["back_copied"], 1)
                for t in range(1, 16, 2):
                    dve.wait_ge(S["t_turned"], n * 16 + t + 1)
                    v.tensor_copy(work_r[0:T, t // 4, 512 * (t % 4):512 * (t % 4) + 512], ps[0:T, t % 4, :])\
                        .then_inc(S["t_turned_dve"], 1)
                for u, (c, m, w, i) in enumerate(FINAL_UNITS):
                    dve.wait_ge(S["final"], n * NF + u + 1)
                    y = image[:, c:c + m, 2 * w * i:2 * w * (i + 1)].rearrange("p c (b w) -> p b c w", b=2)
                    o = ps[:, 2 * (u % 4):2 * (u % 4) + 2, 0:w * m].rearrange("p b (c w) -> p b c w", w=w)
                    v.tensor_tensor(y, y, o, ALU.add).then_inc(S["final_out"], 1)
            assert linked[0] - SETUP_LINKS == LINKS, linked[0] - SETUP_LINKS


def kernel(x, L0_conv_w, L0_conv_b, L1_conv_conv1_w, L1_conv_mag_s_w, L1_conv_mag_s_b, L1_conv_mag_f_w,
           L1_conv_mag_f_b, L1_conv_mag_w, L1_conv_mag_b, L1_conv_pha_w, L1_conv_pha_b, L1_conv_conv_0_w,
           L1_conv_conv_0_b, L1_conv_conv_1_w, L1_conv_conv_1_b, L1_conv_conv2_w):
    import concourse.bacc as bacc
    from concourse.bass_utils import run_bass_kernel_spmd

    tables, once, at = constant_tables()
    row = lambda a: np.ascontiguousarray(a).reshape(1, -1)
    col = lambda a: np.ascontiguousarray(a).reshape(-1, 1)
    turned = lambda a: np.ascontiguousarray(np.asarray(a).T)
    arrays = dict(
        x=np.ascontiguousarray(x), tables=tables, once=once, l0_w=row(L0_conv_w), l0_b=row(L0_conv_b),
        w1=np.ascontiguousarray(L1_conv_conv1_w), w1_t=turned(L1_conv_conv1_w),
        ws=np.ascontiguousarray(L1_conv_mag_s_w).reshape(C0, C0 * 9), ws_b=col(L1_conv_mag_s_b),
        wf_in=np.ascontiguousarray(L1_conv_mag_f_w), wf_b=col(L1_conv_mag_f_b),
        ww_t=turned(L1_conv_mag_w), ww_b=row(L1_conv_mag_b), wp_t=turned(L1_conv_pha_w), wp_b=row(L1_conv_pha_b),
        w0_t=turned(L1_conv_conv_0_w), w0_b=row(L1_conv_conv_0_b),
        wc_t=turned(L1_conv_conv_1_w), wc_b=row(L1_conv_conv_1_b), w2_t=turned(L1_conv_conv2_w))
    nc = bacc.Bacc("TRN2", target_bir_lowering=False, num_devices=1)
    nc.disable_value_cache = True
    aps = {k: nc.dram_tensor(k, a.shape, mybir.dt.float32, kind="ExternalInput").ap() for k, a in arrays.items()}
    out = nc.dram_tensor("out", arrays["x"].shape, mybir.dt.float32, kind="ExternalOutput").ap()
    build(nc, at=at, out=out, **aps)
    return run_bass_kernel_spmd(nc, [arrays], core_ids=[0]).results[0]["out"]
```

```python
import math
from contextlib import ExitStack

import numpy as np
import concourse.bass as bass
from concourse import mybir

N, C, H, W = 16, 192, 128, 128
G, CG = 32, 6
Q = 4
LOADS = 4
GQ, CQ = G // Q, C // Q
C1, C0 = C // 4, C // 12
HALF = C // 2
KW = W // 2 + 1
LO = (H - int(H * math.cos(math.pi / 4))) // 2
BOX = int(H * math.cos(math.pi / 4))
WB = 8
WO = WB - 2
NBOX = BOX // WO
T = 2 * (C1 + 1)
EPS = 1e-5
ROUND = 12582912.0
TWO_PI = 6.283185
assert BOX % WO == 0


def frft_matrices():
    n_ = W

    def fftconv(a, kern):
        length = a.shape[-1] + kern.shape[0] - 1
        return np.fft.ifft(np.fft.fft(a, n=length, axis=-1) * np.fft.fft(kern, n=length), axis=-1)

    def chirp(f, a):
        alpha = a * math.pi / 2
        tana2, sina = math.tan(alpha / 2), math.sin(alpha)
        y = np.zeros(f.shape[:-1] + (2 * n_ - 1,), np.complex128)
        y[..., ::2] = f
        fi = fftconv(y, np.sinc(np.arange(-(2 * n_ - 3), 2 * n_ - 2) / 2.0))[..., 2 * n_ - 3:4 * n_ - 4]
        pad = np.zeros(f.shape[:-1] + (n_ - 1,), np.complex128)
        n = np.arange(-2 * n_ + 2, 2 * n_ - 1).astype(np.float64)
        chrp = np.exp(-1j * math.pi / n_ * tana2 / 4 * n ** 2)
        c = math.pi / n_ / sina / 4
        m = np.arange(-(4 * n_ - 4), 4 * n_ - 3).astype(np.float64)
        ret = fftconv(chrp * np.concatenate([pad, fi, pad], axis=-1), np.exp(1j * c * m ** 2))
        ret = chrp * (ret[..., 4 * n_ - 4:8 * n_ - 7] * math.sqrt(c / math.pi))
        return np.exp(-1j * (1 - a) * math.pi / 4) * ret[..., n_ - 1:3 * n_ - 2:2]

    eye = np.eye(n_, dtype=np.complex128)
    forward = chirp(eye, 0.5)
    shift = (np.arange(n_) + n_ // 2) % n_
    centred = (np.fft.ifft(eye[..., shift], axis=-1) * math.sqrt(n_))[..., np.argsort(shift)]
    return forward, chirp(centred, 0.5)


def triple(m):
    return np.concatenate([-m.imag, m.real, m.imag], 1)


def constant_tables():
    fwd, inv = frft_matrices()
    j = np.arange(128)
    turn = np.outer(j, j) % 128
    cos, sin = np.cos(2 * np.pi * turn / 128), np.sin(2 * np.pi * turn / 128)
    cos[turn % 64 == 32] = 0
    sin[turn % 64 == 0] = 0
    dft = cos - 1j * sin
    wgt = np.full(KW, 2.0)
    wgt[[0, KW - 1]] = 1.0
    tab = {}
    tab["frft"] = triple(fwd)
    tab["ifrft"] = triple(inv)
    tab["dft_h"] = np.concatenate([dft.real, dft.imag], 1)
    tab["dft_w"] = triple(dft[:, :KW])
    tab["idft_h"] = triple(np.conj(dft) / H)
    top = np.zeros((128, 128))
    top[:KW] = cos[:KW] * wgt[:, None] / W
    tab["idft_w_re"] = top
    top = np.zeros((128, 128))
    top[:KW] = -sin[:KW] * wgt[:, None] / W
    tab["idft_w_im"] = top
    tab["ident"] = np.eye(128)
    tab["average"] = np.full((128, 128), 1.0 / 128)
    rows = np.zeros((128, 2))
    rows[LO:LO + BOX, 0] = 1
    rows[:, 1] = 1 - rows[:, 0]
    tab["rows"] = rows
    edge = np.ones((128, 2))
    edge[:C0, 0] = 0
    edge[(WB - 1) * C0:, 1] = 0
    tab["edge"] = edge
    lane12 = np.zeros((128, 2 * CG))
    lane12[[C1, 2 * C1 + 1]] = np.tile(np.eye(2), (1, CG))
    tab["lane12"] = lane12
    keep = np.ones((128, 1))
    keep[[C1, 2 * C1 + 1]] = 0
    tab["keep"] = keep
    member = np.zeros((128, 2, G))
    for c in range(HALF):
        for h in range(2):
            member[c, h, (h * HALF + c) // CG] = 1
    tab["member"] = member.reshape(128, 2 * G)
    once = {}
    for k in range(3):
        once[f"band{k}"] = np.eye(128, k=1 - k)
    once["lane"] = np.kron(np.eye(WB), np.ones((C0, 1)))
    for k in range(3):
        once[f"tap{k}"] = np.kron(np.eye(WB, WO, k=-k), np.ones((C0, 1)))
    spread = np.zeros((128, 128))
    spread[:C0] = np.kron(np.ones((1, WB)), np.eye(C0))
    once["spread"] = spread
    spread = np.zeros((128, 128))
    spread[:C1, :T] = np.kron(np.ones((1, 2)), np.eye(C1, C1 + 1))
    once["spread2"] = spread
    lane2 = np.zeros((128, 2))
    lane2[:T] = np.kron(np.eye(2), np.ones((C1 + 1, 1)))
    once["lane2"] = lane2
    at, packed = {}, []
    for tables in (tab, once):
        start = 0
        for name, t in tables.items():
            at[name] = (start, t.shape[1], tables is once)
            start += t.shape[1]
        packed.append(np.concatenate(list(tables.values()), 1).astype(np.float32))
    return packed[0], packed[1], at


def build(nc, x, tables, once, at, l0_w, l0_b, w1, w1_t, ws, ws_b, wf_in, wf_b, ww_t, ww_b,
          wp_t, wp_b, w0_t, w0_b, wc_t, wc_b, w2_t, out):
    f32 = mybir.dt.float32
    ALU = mybir.AluOpType
    ACT = mybir.ActivationFunctionType
    AX = mybir.AxisListType
    ctx = ExitStack()
    with ctx:
        def sb(name, shape):
            return ctx.enter_context(nc.sbuf_tensor(name, shape, f32))

        def sem(name):
            return ctx.enter_context(nc.semaphore(name))

        image = sb("image", [128, C, W])
        mix = sb("mix", [128, W, C1 + 1])
        work_r = sb("work_r", [128, 4, C0 * W])
        FT = len(range(0, KW, WB)) * 128
        work_f = sb("work_f", [128, 2 * FT + 2 * C0 * KW])
        boxed = sb("boxed", [128, NBOX, H + 2])
        hop = sb("hop", [128, 4, 512])
        table = sb("table", [128, sum(k for _, k, o in at.values() if not o)])
        once_sb = work_r[:, 0, 0:sum(k for _, k, o in at.values() if o)]
        ps = ctx.enter_context(nc.psum_tensor("ps", [128, 8, 512], f32))

        def tab(name, rows=128):
            s, k, o = at[name]
            return once_sb[0:rows, s:s + k] if o else table[0:rows, s:s + k]

        def real_row(name):
            k = at[name][1] // 3
            return tab(name)[:, k:3 * k]

        def imag_row(name):
            k = at[name][1] // 3
            return tab(name)[:, 0:2 * k]

        wraw0 = sb("wraw0", [128, 10])
        band = sb("band", [128, 3, 128])
        w1t_sb = sb("w1t_sb", [HALF, 2, C1])
        w1s = sb("w1s", [HALF, 2, C1])
        blk_s = sb("blk_s", [128, 3, C0 * WO])
        blk_f = sb("blk_f", [128, C0 * WB])
        blk_p = sb("blk_p", [128, C0 * WB])
        blk_c = sb("blk_c", [128, C0 * WB])
        blk_o = sb("blk_o", [128, C, 2])
        bias_s = sb("bias_s", [128, C0])
        bias_f = sb("bias_f", [128, C0])
        bias_in = sb("bias_in", [128, C0])
        bias_p = sb("bias_p", [128, C0])
        bias_c = sb("bias_c", [128, C0])
        bias_q = sb("bias_q", [128, C0])
        bias_0 = sb("bias_0", [128, C1])
        bias_1 = sb("bias_1", [128, C1])
        eps_t = sb("eps_t", [128, 1])
        half_pi = sb("half_pi", [128, 1])
        parts = sb("parts", [128, GQ, 12])
        xmv = sb("xmv", [128, 2, GQ, 2])
        ymv = sb("ymv", [128, G, 2])
        dev = sb("dev", [128, G])
        mean0 = sb("mean0", [128, G])
        nmean0 = sb("nmean0", [128, G])
        rstd0 = sb("rstd0", [128, G])
        mean1 = sb("mean1", [128, G])
        rstd1 = sb("rstd1", [128, G])
        tiny = sb("tiny", [128, G])
        prod = sb("prod", [HALF, 2, 2, G])
        col1 = sb("col1", [HALF, 2, 2])
        mrep = hop[0:HALF, 0, 0:2 * 128].rearrange("p (s h) -> p s h", s=2)
        const_o = hop[:, 1, 0:2 * C].rearrange("p (c w) -> p c w", w=2)
        yparts = sb("yparts", [128, GQ, 12])
        scratch = sb("scratch", [128, 1])
        newt = sb("newt", [128, G])

        raw = work_r[:, 3, :]
        off = [0]

        def take(rows, cols):
            s = off[0]
            off[0] += cols
            return raw[0:rows, s:s + cols]

        r_ws = take(C0, C0 * 9)
        r_wf = take(C0, C0)
        r_ww = take(C0, C0)
        r_wp = take(C0, C0)
        r_w0 = take(C0, C0)
        r_wc = take(C0, C0)
        r_w1 = take(C0, C)
        r_w2 = take(C1, C)
        r_bs = take(C0, 1)
        r_bf = take(C0, 1)
        r_bw = take(128, C0)
        r_bp = take(128, C0)
        r_bc = take(128, C0)
        r_b0 = take(128, C0)
        r_bsr = take(C0, 128)
        r_bfr = take(C0, 128)
        r_sp = take(C0, C0 * 9)
        r_fp = take(C0, C0)
        s_exp = work_r[:, 2, 0:C0 * 9]
        f_exp = work_r[:, 2, 256:256 + C0]
        p_exp = work_r[:, 2, 272:272 + C0]
        c_exp = work_r[:, 2, 288:288 + C0]
        s_tmp = work_r[:, 2, 512:512 + C0 * WO]

        S = {k: sem(k) for k in (
            "weights_in", "setup_dve", "setup_pe", "ones_set",
            "x_parts", "x_mean", "x_dev", "x_var", "x_sd", "x_rstd", "centred", "conv", "y_out",
            "y_parts", "y_mean", "y_dev", "y_var", "y_sd", "mix_w", "mix_bias", "mix_ready",
            "y_turned", "turned_a", "turned_b", "mixed", "mix_out",
            "plane_1", "plane_1_out", "plane_2", "plane_2_out_r", "plane_2_out_f",
            "squares", "square_sum", "magnitude", "inverse", "tangent", "arctan", "sign", "corner", "fold", "phase",
            "turned", "turned_out", "box_turned", "box_turned_out", "mag_mixed", "mixed_out",
            "box_mixed", "box_mixed_out", "whole", "fraction", "sine", "z_im", "z_re",
            "back_1", "back_1_out", "back_2", "back_squares", "back_copied",
            "abs_sum", "abs_done", "t_turned", "t_turned_act", "t_turned_dve", "final", "final_out", "link")}
        loaded = [[sem(f"loaded{q}_{i}") for i in range(LOADS)] for q in range(Q)]
        stored = [[sem(f"stored{q}_{i}") for i in range(LOADS)] for q in range(Q)]

        x_v = x.rearrange("n c h w -> n h c w")
        out_v = out.rearrange("n c h w -> n h c w")

        def parts_of(q):
            step = CQ // LOADS
            return [slice(q * CQ + i * step, q * CQ + (i + 1) * step) for i in range(LOADS)]

        def group(g):
            return slice(g * CG, (g + 1) * CG)

        PAIRS = C0 // 2
        FIRST, COLS = (C0, 2 * C0), (W, KW)

        def buf(k, i):
            if k == 0:
                return work_r[:, i, :]
            s = i * FT if i < 2 else 2 * FT + (i - 2) * C0 * KW
            return work_f[:, s:s + C0 * KW]

        def planes_of(k, i):
            return buf(k, i)[:, 0:C0 * COLS[k]].rearrange("p (w c) -> p c w", c=C0)

        def re_im(k):
            both = work_r[:, 0:2, :] if k == 0 else work_f[:, 0:2 * FT].rearrange("p (r x) -> p r x", r=2)
            return both[:, :, 0:C0 * COLS[k]].rearrange("p r (w c) -> p r c w", c=C0)

        LOTS = [(0, 4 * i, 4 * i + 4) for i in range(4)] + [(1, 0, 8), (1, 8, 16)]
        NL = len(LOTS)

        def lot(j, i):
            k, a, b = LOTS[j]
            return buf(k, i)[:, 0:C0 * COLS[k]].rearrange("p (w c) -> p w c", c=C0)[:, :, a:b]

        SLICES = [(0, 0, 32), (0, 32, 64), (0, 64, 96), (0, 96, 128), (1, 0, 32), (1, 32, KW)]
        NS = len(SLICES)

        def sl(j, i):
            k, a, b = SLICES[j]
            return buf(k, i)[:, C0 * a:C0 * b]

        UNITS = [(0, 32 * t, 4) for t in range(4)] + [(1, 0, 4), (1, 32, 4), (1, KW - WB, 1)]
        NU = len(UNITS)

        def turned_at(j, m):
            k, a, blocks = UNITS[j]
            s = (a // WB if blocks == 4 else 8) * 128
            if k == 0:
                return work_r[:, m, s:s + blocks * 128]
            return work_f[:, m * FT + s:m * FT + s + blocks * 128]

        FINAL = [(c, C // 3, 8) for c in range(0, C, C // 3)]
        FINAL_UNITS = [(c, m, w, v) for c, m, w in FINAL for v in range(W // (2 * w))]
        NF = len(FINAL_UNITS)
        READY = (8, 16, 24, 24)

        FINAL_BANK = (4, 6, 0, 2)
        CONV_BANK = (0, 2, 6)
        PLANE_BANK = (0, 1, 6, 7)

        block = ctx.enter_context(nc.Block())

        @block.sync
        def _(sp):
            for dst, src in ((table[:], tables[:]), (once_sb, once[:]), (wraw0[:, 0:9], l0_w.broadcast_to([128, 9])), (wraw0[:, 9:10], l0_b.broadcast_to([128, 1])),
                             (w1t_sb[:], w1_t.rearrange("(s c) o -> c s o", s=2)),
                             (r_ws, ws), (r_wf, wf_in), (r_ww, ww_t), (r_wp, wp_t), (r_w0, w0_t), (r_wc, wc_t),
                             (r_w1, w1[0:C0, :]), (r_w2, w2_t), (r_bs, ws_b), (r_bf, wf_b),
                             (r_bw, ww_b.broadcast_to([128, C0])), (r_bp, wp_b.broadcast_to([128, C0])), (r_bc, wc_b.broadcast_to([128, C0])), (r_b0, w0_b.broadcast_to([128, C0]))):
                sp.dma_start(dst, src).then_inc(S["weights_in"], 16)
            for q in range(Q):
                for i, c in enumerate(parts_of(q)):
                    sp.dma_start(image[:, c, :], x_v[0, :, c, :]).then_inc(loaded[q][i], 16)
            with sp.Fori(0, N - 1) as n:
                for q0, qs in ((0, (0,)), (1, (1,)), (2, (2, 3))):
                    sp.wait_ge(S["final_out"], n * NF + READY[q0])
                    for q in qs:
                        for i, c in enumerate(parts_of(q)):
                            sp.dma_start(out_v[n, :, c, :], image[:, c, :]).then_inc(stored[q][i], 16)
                    for q in qs:
                        for i, c in enumerate(parts_of(q)):
                            sp.wait_ge(stored[q][i], n * 16 + 16)
                            sp.dma_start(image[:, c, :], x_v[n + 1, :, c, :]).then_inc(loaded[q][i], 16)
            for q in range(Q):
                sp.wait_ge(S["final_out"], (N - 1) * NF + READY[q])
                for i, c in enumerate(parts_of(q)):
                    sp.dma_start(out_v[N - 1, :, c, :], image[:, c, :]).then_inc(stored[q][i], 16)
            for q in range(Q):
                for i in range(LOADS):
                    sp.wait_ge(stored[q][i], N * 16)

        @block.tensor
        def _(pe):
            mm, turn = nc.tensor.matmul, nc.tensor.transpose
            ident = tab("ident")
            pe.wait_ge(S["setup_dve"], 1)
            for half in range(2):
                mm(ps[0:HALF, 0, half * C0:(half + 1) * C0], r_w1[:, half * HALF:(half + 1) * HALF], r_w0,
                   start=half == 0, stop=True, skip_group_check=True)
            for t in range(9):
                mm(ps[0:C0, 1, t * C0:(t + 1) * C0], r_ws.rearrange("o (c t) -> o t c", t=9)[:, t, :], r_ww,
                   start=t == 0, stop=True, skip_group_check=True)
            mm(ps[0:C0, 2, 0:C0], r_wf, r_ww, start=True, stop=True)
            mm(ps[:, 3, 0:C0], r_bsr, r_ww, start=True, stop=True)
            mm(ps[:, 4, 0:C0], r_bfr, r_ww, start=True, stop=True)
            mm(ps[0:T, 5, 0:C], tab("spread2", C1)[:, 0:T], r_w2, start=True, stop=True)
            mm(ps[:, 6, 0:C0], tab("spread", C0), r_wp, start=True, stop=True)
            mm(ps[:, 7, 0:C0], tab("spread", C0), r_wc, start=True, stop=True).then_inc(S["setup_pe"], 1)
            pe.wait_ge(S["setup_dve"], 2)
            mm(ps[:, 0, 0:C0 * 9], tab("spread", C0), r_sp, start=True, stop=True)
            mm(ps[:, 1, 0:C0], tab("spread", C0), r_fp, start=True, stop=True).then_inc(S["setup_pe"], 1)
            pe.wait_ge(S["setup_dve"], 3)

            def x_average(n, q):
                pe.wait_ge(S["x_parts"], n * Q + q + 1)
                mm(ps[:, 4, 0:GQ], tab("average"), xmv[:, q % 2, :, 0], start=True, stop=True)\
                    .then_inc(S["x_mean"], 1)

            def x_variance(n, q):
                pe.wait_ge(S["x_dev"], n * Q + q + 1)
                mm(ps[:, 5, 0:GQ], tab("average"), dev[:, 0:GQ], start=True, stop=True)\
                    .then_inc(S["x_var"], 1)

            def conv(n, g):
                pe.wait_ge(S["centred"], n * G + g + 1)
                if g >= 3:
                    pe.wait_ge(S["y_out"], n * G + g - 2)
                for j in range(2):
                    c = slice(g * CG + 3 * j, g * CG + 3 * j + 3)
                    o = ps[:, CONV_BANK[g % 3] + j, 0:3 * W].rearrange("p (c w) -> p c w", c=3)
                    mm(o, band[:, 1, :], image[:, c, :], start=True, stop=False)
                    mm(o[:, :, 1:W], band[:, 0, :], image[:, c, 0:W - 1], start=False, stop=False)
                    last = mm(o[:, :, 0:W - 1], band[:, 2, :], image[:, c, 1:W], start=False, stop=True)
                last.then_inc(S["conv"], 1)

            with pe.Fori(0, N) as n:
                x_average(n, 0)
                x_variance(n, 0)
                for q in range(Q):
                    for g in range(GQ):
                        conv(n, q * GQ + g)
                        if q + 1 < Q and g == 4:
                            x_average(n, q + 1)
                        if q + 1 < Q and g == 5:
                            x_variance(n, q + 1)
                pe.wait_ge(S["y_parts"], n + 1)
                mm(ps[:, 0, 0:G], tab("average"), ymv[:, :, 0], start=True, stop=True).then_inc(S["y_mean"], 1)
                pe.wait_ge(S["y_dev"], n + 1)
                mm(ps[:, 1, 0:G], tab("average"), dev[:], start=True, stop=True).then_inc(S["y_var"], 1)

                def mix_block(b):
                    pe.wait_ge(S["turned_a"], n * 32 + b + 1)
                    pe.wait_ge(S["turned_b"], n * 32 + b + 1)
                    if b == 2:
                        pe.wait_ge(S["mix_ready"], n + 1)
                    if b % 2 == 0 and b >= 4:
                        pe.wait_ge(S["mix_out"], n * 16 + b // 2 - 1)
                    for i in range(4):
                        o = ps[:, (b // 2) % 2, ((b % 2) * 4 + i) * C1:((b % 2) * 4 + i + 1) * C1]
                        for half in range(2):
                            last = mm(o, work_r[0:HALF, b % 4, (4 * half + i) * 128:(4 * half + i + 1) * 128],
                                      w1s[:, half, :], start=half == 0, stop=half == 1)
                    last.then_inc(S["mixed"], 1)

                def turn_columns(b):
                    if b >= 3:
                        pe.wait_ge(S["turned_a"], n * 32 + b - 2)
                        pe.wait_ge(S["turned_b"], n * 32 + b - 2)
                    for half in range(2):
                        for i in range(4):
                            last = turn(ps[0:HALF, 2 + 2 * (b % 3) + half, i * 128:(i + 1) * 128],
                                        image[:, half * HALF:(half + 1) * HALF, 4 * b + i], ident)
                    last.then_inc(S["y_turned"], 1)

                for b in range(3):
                    turn_columns(b)
                pe.wait_ge(S["mix_w"], n + 1)
                for half in range(2):
                    last = mm(ps[:, 1, 64:64 + C1], mrep[:, half, :], w1s[:, half, :], start=half == 0, stop=half == 1)
                last.then_inc(S["mix_bias"], 1)
                for b in range(3, 32):
                    mix_block(b - 3)
                    turn_columns(b)
                for b in range(29, 32):
                    mix_block(b)
                pe.wait_ge(S["mix_out"], n * 16 + 16)

                def plane_1(u):
                    k, p = divmod(u, PAIRS)
                    if u >= 4:
                        pe.wait_ge(S["plane_1_out"], n * 2 * PAIRS + u - 3)
                    for i in range(2):
                        last = mm(ps[:, PLANE_BANK[u % 4], i * 256:(i + 1) * 256], mix[:, :, FIRST[k] + 2 * p + i],
                                  tab("dft_h") if k else real_row("frft"), start=True, stop=True)
                    last.then_inc(S["plane_1"], 1)

                def plane_2(u):
                    k, cols = u // PAIRS, COLS[u // PAIRS]
                    name = "dft_w" if k else "frft"
                    pe.wait_ge(S["plane_1_out"], n * 2 * PAIRS + u + 1)
                    if u >= 4:
                        if u - 4 < PAIRS:
                            pe.wait_ge(S["plane_2_out_r"], n * PAIRS + u - 3)
                        else:
                            pe.wait_ge(S["plane_2_out_f"], n * PAIRS + u - 3 - PAIRS)
                    for i in range(2):
                        o = ps[:, 2 + u % 4, i * 2 * cols:(i + 1) * 2 * cols]
                        a = hop[:, u % 4, i * 256:(i + 1) * 256]
                        mm(o, a[:, 0:128], real_row(name), start=True, stop=False)
                        last = mm(o, a[:, 128:256], imag_row(name), start=False, stop=True)
                    last.then_inc(S["plane_2"], 1)

                for u in range(2 * PAIRS):
                    plane_1(u)
                    if u >= 2:
                        plane_2(u - 2)
                plane_2(2 * PAIRS - 2)
                plane_2(2 * PAIRS - 1)
                pe.wait_ge(S["plane_2_out_f"], n * PAIRS + PAIRS)

                def turn_unit(j):
                    k, a, blocks = UNITS[j]
                    pe.wait_ge(S["phase"], n * NL + (NL if k else 4))
                    if j >= 1:
                        pe.wait_ge(S["turned_out"], n * NU + j)
                    for m in range(2):
                        for i in range(blocks):
                            c = C0 * (a + WB * i)
                            last = turn(ps[:, 4 + m, i * 128:(i + 1) * 128], buf(k, 2 + m)[:, c:c + C0 * WB], ident)
                    last.then_inc(S["turned"], 1)

                def mix_unit(j):
                    k, a, blocks = UNITS[j]
                    pe.wait_ge(S["turned_out"], n * NU + j + 1)
                    if j >= 1:
                        pe.wait_ge(S["mixed_out"], n * NU + j)
                    for m, weights in enumerate((blk_c, blk_c) if k else (blk_f, blk_p)):
                        for i in range(blocks):
                            last = mm(ps[:, 6 + m, i * 128:(i + 1) * 128],
                                      turned_at(j, m)[:, i * 128:(i + 1) * 128], weights[:], start=True, stop=True)
                    last.then_inc(S["mag_mixed"], 1)

                def turn_box(t):
                    if t >= 2:
                        pe.wait_ge(S["box_turned_out"], n * 4 + t - 1)
                    for i, j in enumerate(range(4 * t, min(4 * t + 4, NBOX))):
                        c = C0 * (LO - 1 + WO * j)
                        last = turn(ps[:, t % 2, i * 128:(i + 1) * 128], work_r[:, 2, c:c + C0 * WB], ident)
                    last.then_inc(S["box_turned"], 1)

                def conv_box(t):
                    pe.wait_ge(S["box_turned_out"], n * 4 + t + 2)
                    for i in range(5):
                        o = ps[:, (2 + t) % 4, i * C0 * WO:(i + 1) * C0 * WO]
                        for dy in range(3):
                            last = mm(o, boxed[:, 5 * t + i, dy:dy + 128], blk_s[:, dy, :],
                                      start=dy == 0, stop=dy == 2)
                    last.then_inc(S["box_mixed"], 1)

                turn_unit(0)
                turn_unit(1)
                turn_box(0)
                mix_unit(0)
                turn_unit(2)
                turn_box(1)
                turn_box(2)
                mix_unit(1)
                turn_unit(3)
                turn_box(3)
                conv_box(0)
                mix_unit(2)
                conv_box(1)
                mix_unit(3)
                conv_box(2)

                def back_1(u):
                    k, p = divmod(u, PAIRS)
                    cols, name = COLS[k], "idft_h" if k else "ifrft"
                    if u == 0:
                        pe.wait_ge(S["z_re"], n * NS + 4)
                        pe.wait_ge(S["z_im"], n * NS + 4)
                    if u == PAIRS:
                        pe.wait_ge(S["z_re"], n * NS + NS)
                        pe.wait_ge(S["z_im"], n * NS + NS)
                    if u >= 2:
                        pe.wait_ge(S["back_1_out"], n * 2 * PAIRS + u - 1)
                    for i in range(2):
                        o = ps[0:cols, u % 2, i * 256:(i + 1) * 256]
                        mm(o, planes_of(k, 0)[:, 2 * p + i, :], real_row(name), start=True, stop=False)
                        last = mm(o, planes_of(k, 1)[:, 2 * p + i, :], imag_row(name), start=False, stop=True)
                    last.then_inc(S["back_1"], 1)

                def back_2(u):
                    k, cols = u // PAIRS, COLS[u // PAIRS]
                    pe.wait_ge(S["back_1_out"], n * 2 * PAIRS + u + 1)
                    if u >= 2 and u - 2 < PAIRS:
                        pe.wait_ge(S["back_squares"], n * PAIRS + u - 1)
                    elif u >= 2:
                        pe.wait_ge(S["back_copied"], n * PAIRS + u - 1 - PAIRS)
                    re, im = (tab("idft_w_re", KW), tab("idft_w_im", KW)) if k else (real_row("ifrft"), imag_row("ifrft"))
                    wide = 128 if k else 256
                    for i in range(2):
                        a = hop[0:cols, u % 2, i * 256:(i + 1) * 256]
                        o = ps[:, 2 + u % 2, i * wide:(i + 1) * wide]
                        mm(o, a[:, 0:128], re, start=True, stop=False)
                        last = mm(o, a[:, 128:256], im, start=False, stop=True)
                    last.then_inc(S["back_2"], 1)

                for u in range(2 * PAIRS):
                    if u == PAIRS:
                        back_2(u - 1)
                    back_1(u)
                    if u >= 1 and u != PAIRS:
                        back_2(u - 1)
                    if u == 1:
                        turn_unit(4)
                    if u == 2:
                        mix_unit(4)
                        turn_unit(5)
                    if u == 3:
                        turn_unit(6)
                        mix_unit(5)
                    if u == 4:
                        mix_unit(6)
                back_2(2 * PAIRS - 1)
                pe.wait_ge(S["back_copied"], n * PAIRS + PAIRS)

                pe.wait_ge(S["abs_done"], n + 1)
                for t in range(16):
                    if t >= 4:
                        pe.wait_ge(S["t_turned_act" if t % 2 == 0 else "t_turned_dve"], n * 8 + t // 2 - 1)
                    for i in range(4):
                        j = 4 * t + i
                        last = turn(ps[0:T, t % 4, i * 128:(i + 1) * 128], mix[:, 2 * j:2 * j + 2, :], ident)
                    last.then_inc(S["t_turned"], 1)
                turned = work_r[:].rearrange("p a (b h) -> p (a b) h", h=128)
                for u, (c, m, w, v) in enumerate(FINAL_UNITS):
                    if u < 4:
                        for name in ("t_turned_act", "t_turned_dve"):
                            pe.wait_ge(S[name], n * 8 + (u + 1 if u < 2 else u + 5))
                    if u >= 4:
                        pe.wait_ge(S["final_out"], n * NF + u - 3)
                    for bank in range(2):
                        o = ps[:, FINAL_BANK[u % 4] + bank, 0:w * m].rearrange("p (c w) -> p c w", w=w)
                        for i in range(w // 2):
                            last = mm(o[:, :, 2 * i:2 * i + 2], turned[0:T, (2 * v + bank) * (w // 2) + i, :],
                                      blk_o[0:T, c:c + m, :], start=i == 0, stop=True, skip_group_check=True)
                    last.then_inc(S["final"], 1)

        @block.scalar
        def _(act):
            act.wait_ge(S["setup_dve"], 3)
            with act.Fori(0, N) as n:
                def centre(g):
                    nc.scalar.activation(image[:, group(g), :], image[:, group(g), :], ACT.Identity,
                                         bias=nmean0[:, g:g + 1]).then_inc(S["centred"], 1)

                def x_sd(q):
                    act.wait_ge(S["x_var"], n * Q + q + 1)
                    nc.scalar.activation(tiny[:, 0:GQ], ps[:, 5, 0:GQ], ACT.Sqrt, bias=eps_t[:]).then_inc(S["x_sd"], 1)

                act.wait_ge(S["x_dev"], n * Q + 1)
                centre(0)
                x_sd(0)
                for q in range(Q):
                    if q:
                        act.wait_ge(S["x_rstd"], n * Q + q + 1)
                    for g in range(0 if q else 1, GQ):
                        centre(q * GQ + g)
                    if q + 1 < Q:
                        x_sd(q + 1)
                act.wait_ge(S["y_var"], n + 1)
                nc.scalar.activation(tiny[:], ps[:, 1, 0:G], ACT.Sqrt, bias=eps_t[:]).then_inc(S["y_sd"], 1)
                for b in range(32):
                    act.wait_ge(S["y_turned"], n * 32 + b + 1)
                    if b >= 4:
                        act.wait_ge(S["mixed"], n * 32 + b - 3)
                    nc.scalar.copy(work_r[0:HALF, b % 4, 0:512], ps[0:HALF, 2 + 2 * (b % 3), :]).then_inc(S["turned_a"], 1)
                act.wait_ge(S["mixed"], n * 32 + 32)

                pa = n * 2 * PAIRS

                def plane_1_out(u):
                    act.wait_ge(S["plane_1"], pa + u + 1)
                    if u >= 4:
                        act.wait_ge(S["plane_2"], pa + u - 3)
                    nc.scalar.copy(hop[:, u % 4, :], ps[:, PLANE_BANK[u % 4], :]).then_inc(S["plane_1_out"], 1)

                def plane_2_out(u):
                    p = u - PAIRS
                    act.wait_ge(S["plane_2"], pa + u + 1)
                    nc.scalar.copy(re_im(1)[:, :, 2 * p:2 * p + 2, :],
                                   ps[:, 2 + u % 4, 0:4 * KW].rearrange("p (c r w) -> p r c w", c=2, r=2))\
                        .then_inc(S["plane_2_out_f"], 1)

                def squares(j):
                    k, a, b = LOTS[j]
                    act.wait_ge(S["plane_2_out_f" if k else "plane_2_out_r"], n * PAIRS + b // 2)
                    nc.scalar.activation(lot(j, 2), lot(j, 0), ACT.Square)
                    nc.scalar.activation(lot(j, 3), lot(j, 1), ACT.Square).then_inc(S["squares"], 1)

                def magnitude(j):
                    act.wait_ge(S["square_sum"], n * NL + j + 1)
                    nc.scalar.activation(lot(j, 2), lot(j, 2), ACT.Sqrt)
                    nc.scalar.activation(lot(j, 3), lot(j, 0), ACT.Abs).then_inc(S["magnitude"], 1)

                def arctan(j):
                    act.wait_ge(S["tangent"], n * NL + j + 1)
                    nc.scalar.activation(lot(j, 3), lot(j, 3), ACT.Arctan).then_inc(S["arctan"], 1)

                def turned_out(j):
                    blocks = UNITS[j][2]
                    act.wait_ge(S["turned"], n * NU + j + 1)
                    nc.scalar.copy(turned_at(j, 0), ps[:, 4, 0:blocks * 128])
                    nc.scalar.mul(turned_at(j, 1), ps[:, 5, 0:blocks * 128], -2 / math.pi).then_inc(S["turned_out"], 1)

                def sine(j):
                    act.wait_ge(S["fraction"], n * NS + j + 1)
                    nc.scalar.activation(sl(j, 1), sl(j, 0), ACT.Sin, scale=TWO_PI)
                    nc.scalar.activation(sl(j, 3), sl(j, 0), ACT.Abs).then_inc(S["sine"], 1)
                    act.wait_ge(S["sine"], (n * NS + j) * 2 + 1)
                    nc.scalar.activation(sl(j, 3), sl(j, 3), ACT.Sin, scale=-TWO_PI, bias=half_pi[:]).then_inc(S["sine"], 1)

                for u in range(2 * PAIRS):
                    plane_1_out(u)
                    if u >= PAIRS + 2:
                        plane_2_out(u - 2)
                    if u in (4, 6, 8):
                        squares((u - 4) // 2)
                        magnitude((u - 4) // 2)
                    if u == 10:
                        squares(3)
                    if u == 11:
                        magnitude(3)
                        arctan(0)
                        arctan(1)
                    if u == 14:
                        squares(4)
                arctan(2)
                plane_2_out(2 * PAIRS - 2)
                arctan(3)
                plane_2_out(2 * PAIRS - 1)
                magnitude(4)
                squares(5)
                turned_out(0)
                magnitude(5)
                turned_out(1)
                turned_out(2)
                arctan(4)
                arctan(5)
                turned_out(3)
                for j in range(4):
                    sine(j)

                def back_1_out(u):
                    cols = COLS[u // PAIRS]
                    act.wait_ge(S["back_1"], pa + u + 1)
                    if u >= 2:
                        act.wait_ge(S["back_2"], pa + u - 1)
                    nc.scalar.copy(hop[0:cols, u % 2, :], ps[0:cols, u % 2, :]).then_inc(S["back_1_out"], 1)

                def back_squares(u):
                    act.wait_ge(S["back_2"], pa + u + 1)
                    if u >= 2:
                        act.wait_ge(S["abs_sum"], n * PAIRS + u - 1)
                    nc.scalar.activation(hop[:, 2 + u % 2, :], ps[:, 2 + u % 2, :], ACT.Square).then_inc(S["back_squares"], 1)

                for u in range(2 * PAIRS):
                    if u == PAIRS:
                        back_squares(u - 1)
                    back_1_out(u)
                    if 1 <= u < PAIRS:
                        back_squares(u - 1)
                    if 1 <= u <= 3:
                        turned_out(3 + u)
                    if u in (5, 6):
                        sine(u - 1)
                    if u == PAIRS + 2:
                        act.wait_ge(S["abs_sum"], n * PAIRS + PAIRS)
                        nc.scalar.activation(mix[:, :, C0:2 * C0], mix[:, :, C0:2 * C0], ACT.Sqrt).then_inc(S["abs_done"], 1)
                for t in range(0, 16, 2):
                    act.wait_ge(S["t_turned"], n * 16 + t + 1)
                    nc.scalar.copy(work_r[0:T, t // 4, 512 * (t % 4):512 * (t % 4) + 512], ps[0:T, t % 4, :])\
                        .then_inc(S["t_turned_act"], 1)

        @block.gpsimd
        def _(pool):
            pool.memset(mix[:, :, C1:C1 + 1], 1.0).then_inc(S["ones_set"], 1)
            with pool.Fori(0, N) as n:
                def square_sum(j):
                    pool.wait_ge(S["squares"], n * NL + j + 1)
                    nc.gpsimd.tensor_tensor(lot(j, 2), lot(j, 2), lot(j, 3), ALU.add).then_inc(S["square_sum"], 1)

                def tangent(j):
                    pool.wait_ge(S["inverse"], (n * NL + j) * 2 + 2)
                    nc.gpsimd.tensor_tensor(lot(j, 3), lot(j, 1), lot(j, 3), ALU.mult).then_inc(S["tangent"], 1)

                def corner(j):
                    pool.wait_ge(S["sign"], n * NL + j + 1)
                    nc.gpsimd.tensor_tensor(lot(j, 1), lot(j, 1), lot(j, 0), ALU.mult).then_inc(S["corner"], 1)

                def fraction(j):
                    pool.wait_ge(S["whole"], n * NS + j + 1)
                    nc.gpsimd.tensor_tensor(sl(j, 0), sl(j, 3), sl(j, 0), ALU.subtract).then_inc(S["fraction"], 1)

                def z_im(j):
                    pool.wait_ge(S["sine"], (n * NS + j) * 2 + 2)
                    if j < 4:
                        pool.wait_ge(S["box_mixed_out"], n * 3 + min(j + 1, 3))
                    nc.gpsimd.tensor_tensor(sl(j, 1), sl(j, 2), sl(j, 1), ALU.mult).then_inc(S["z_im"], 1)

                square_sum(0)
                square_sum(1)
                tangent(0)
                square_sum(2)
                tangent(1)
                corner(0)
                square_sum(3)
                tangent(2)
                corner(1)
                tangent(3)
                corner(2)
                corner(3)
                square_sum(4)
                square_sum(5)
                tangent(4)
                tangent(5)
                fraction(0)
                fraction(1)
                fraction(2)
                z_im(0)
                z_im(1)
                fraction(3)
                z_im(2)
                z_im(3)
                corner(4)
                corner(5)

                def abs_sum(u):
                    pool.wait_ge(S["back_squares"], n * PAIRS + u + 1)
                    v = hop[:, 2 + u % 2, :].rearrange("p (c r w) -> p c r w", c=2, r=2)
                    nc.gpsimd.tensor_tensor(mix[:, :, C0 + 2 * u:C0 + 2 * u + 2].rearrange("p w c -> p c w"),
                                            v[:, :, 0, :], v[:, :, 1, :], ALU.add).then_inc(S["abs_sum"], 1)

                for u in range(PAIRS):
                    abs_sum(u)
                    if u in (2, 3):
                        fraction(u + 2)
                    if u in (4, 5):
                        z_im(u)

        @block.vector
        def _(dve):
            v = nc.vector
            linked = [0, None, None]

            def link(ins):
                linked[0] += 1
                ins.then_inc(S["link"], 1)
                value = linked[0]
                if linked[1] is not None:
                    value = linked[1] * LINKS + value
                dve.wait_ge(S["link"], value)

            v.memset(eps_t[:], EPS)
            v.memset(half_pi[:], math.pi / 2)
            v.memset(bias_0[:], 0.0)
            dve.wait_ge(S["weights_in"], 19 * 16)
            v.memset(boxed[:], 0.0)
            v.tensor_scalar(r_bsr, tab("average", C0), r_bs, 128.0, ALU.mult, ALU.mult)
            v.tensor_scalar(r_bfr, tab("average", C0), r_bf, 128.0, ALU.mult, ALU.mult).then_inc(S["setup_dve"], 1)
            for kx in range(3):
                link(v.tensor_scalar(band[:, kx, :], tab("band0"), wraw0[:, kx:kx + 1], None, ALU.mult))
                for ky in (1, 2):
                    link(v.scalar_tensor_tensor(band[:, kx, :], tab(f"band{ky}"), wraw0[:, 3 * ky + kx:3 * ky + kx + 1],
                                                band[:, kx, :], ALU.mult, ALU.add))
            dve.wait_ge(S["setup_pe"], 1)
            v.tensor_copy(w1t_sb[:, :, 0:C0], ps[0:HALF, 0, 0:2 * C0].rearrange("p (s o) -> p s o", s=2))
            v.tensor_copy(r_sp, ps[0:C0, 1, 0:9 * C0])
            v.tensor_copy(r_fp, ps[0:C0, 2, 0:C0])
            v.tensor_tensor(bias_s[:], ps[:, 3, 0:C0], r_bw, ALU.add)
            link(v.tensor_tensor(bias_f[:], ps[:, 4, 0:C0], r_bw, ALU.add))
            link(v.tensor_scalar(bias_in[:], bias_s[:], tab("rows")[:, 0:1], None, ALU.mult))
            v.scalar_tensor_tensor(bias_in[:], bias_f[:], tab("rows")[:, 1:2], bias_in[:], ALU.mult, ALU.add)
            v.tensor_copy(p_exp, ps[:, 6, 0:C0])
            v.tensor_copy(c_exp, ps[:, 7, 0:C0])
            v.tensor_copy(bias_c[:], r_bc)
            v.tensor_copy(bias_0[:, 0:C0], r_b0)
            v.tensor_scalar(bias_p[:], r_bp, 1 / (2 * math.pi), None, ALU.mult)
            v.tensor_scalar(bias_q[:], r_bc, 1 / (2 * math.pi), None, ALU.mult)
            link(v.tensor_tensor(blk_o[0:T], ps[0:T, 5, 0:C].rearrange("p (c w) -> p c w", w=1).broadcast_to([T, C, 2]),
                                 tab("lane2", T).rearrange("p (c w) -> p c w", c=1).broadcast_to([T, C, 2]), ALU.mult))
            v.memset(dev[:, 0:1], 0.0).then_inc(S["setup_dve"], 1)
            dve.wait_ge(S["setup_pe"], 2)
            v.tensor_copy(s_exp, ps[:, 0, 0:9 * C0])
            link(v.tensor_copy(f_exp, ps[:, 1, 0:C0]))

            def spread(dst, src, mask, w):
                return v.tensor_tensor(dst.rearrange("p (b o) -> p b o", b=w),
                                       src.rearrange("p (b o) -> p b o", b=1).broadcast_to([128, w, C0]),
                                       mask.rearrange("p (b o) -> p b o", o=1).broadcast_to([128, w, C0]), ALU.mult)

            link(spread(blk_f[:], f_exp, tab("lane"), WB))
            link(spread(blk_c[:], c_exp, tab("lane"), WB))
            link(spread(blk_p[:], p_exp, tab("lane"), WB))
            for ky in range(3):
                link(spread(blk_s[:, ky, :], s_exp[:, 3 * ky * C0:(3 * ky + 1) * C0], tab("tap0"), WO))
                for kx in (1, 2):
                    link(spread(s_tmp, s_exp[:, (3 * ky + kx) * C0:(3 * ky + kx + 1) * C0], tab(f"tap{kx}"), WO))
                    link(v.tensor_tensor(blk_s[:, ky, :], blk_s[:, ky, :], s_tmp, ALU.add))
            dve.wait_ge(S["ones_set"], 1)
            v.memset(dev[:, 0:1], 0.0).then_inc(S["setup_dve"], 1)

            LINKS = 47
            def newton(dst, sd, var, k):
                t = newt[:, 0:k]
                link(v.reciprocal(dst, sd))
                link(v.tensor_tensor(t, dst, dst, ALU.mult))
                link(v.scalar_tensor_tensor(t, var, EPS, t, ALU.add, ALU.mult))
                link(v.tensor_scalar(t, t, -0.5, 1.5, ALU.mult, ALU.add))
                return v.tensor_tensor(dst, dst, t, ALU.mult)

            def x_stats(n, q, g):
                if g % (GQ // LOADS) == 0:
                    dve.wait_ge(loaded[q][g // (GQ // LOADS)], n * 16 + 16)
                for j in range(2):
                    c = (q * GQ + g) * CG + 3 * j
                    linked[2] = v.bn_stats(parts[:, g, 6 * j:6 * j + 6], image[:, c:c + 3, :])

            def x_aggregate(q):
                link(linked[2])
                v.memset(scratch[:], 0.0)
                for g in range(GQ):
                    last = v.bn_aggr(xmv[:, q % 2, g, :], parts[:, g, :])
                last.then_inc(S["x_parts"], 1)

            for g in range(GQ):
                x_stats(0, 0, g)
            x_aggregate(0)
            SETUP_LINKS = linked[0]

            def one_image(n, more):
                linked[0], linked[1] = SETUP_LINKS, n

                def x_dev(q):
                    gs = slice(q * GQ, (q + 1) * GQ)
                    dve.wait_ge(S["x_mean"], n * Q + q + 1)
                    v.tensor_copy(mean0[:, gs], ps[:, 4, 0:GQ])
                    v.tensor_scalar(nmean0[:, gs], ps[:, 4, 0:GQ], -1.0, None, ALU.mult)
                    link(v.tensor_tensor(dev[:, 0:GQ], xmv[:, q % 2, :, 0], ps[:, 4, 0:GQ], ALU.subtract))
                    link(v.tensor_tensor(dev[:, 0:GQ], dev[:, 0:GQ], dev[:, 0:GQ], ALU.mult))
                    v.tensor_tensor(dev[:, 0:GQ], dev[:, 0:GQ], xmv[:, q % 2, :, 1], ALU.add).then_inc(S["x_dev"], 1)

                def x_rstd(q):
                    gs = slice(q * GQ, (q + 1) * GQ)
                    dve.wait_ge(S["x_sd"], n * Q + q + 1)
                    newton(rstd0[:, gs], tiny[:, 0:GQ], ps[:, 5, 0:GQ], GQ).then_inc(S["x_rstd"], 1)

                x_dev(0)
                x_rstd(0)
                dve.wait_ge(S["x_rstd"], n * Q + 1)
                for q in range(Q):
                    for i in range(GQ):
                        g = q * GQ + i
                        if i == GQ - 1:
                            link(last)
                            v.memset(scratch[:], 0.0)
                            for k in range(GQ - 1):
                                v.bn_aggr(ymv[:, q * GQ + k, :], yparts[:, k, :])
                        dve.wait_ge(S["conv"], n * G + g + 1)
                        o = ps[:, CONV_BANK[g % 3]:CONV_BANK[g % 3] + 2, 0:3 * W]
                        y = image[:, group(g), :].rearrange("p (a c) w -> p a (c w)", a=2)
                        v.scalar_tensor_tensor(y, o, rstd0[:, g:g + 1], y, ALU.mult, ALU.add).then_inc(S["y_out"], 1)
                        dve.wait_ge(S["y_out"], n * G + g + 1)
                        for j in range(2):
                            last = v.bn_stats(yparts[:, i, 6 * j:6 * j + 6], image[:, g * CG + 3 * j:g * CG + 3 * j + 3, :])
                        if q + 1 < Q:
                            for k in ((0, 1, 2), (3, 4, 5), (6, 7))[i] if i < 3 else ():
                                x_stats(n, q + 1, k)
                            if i == 2:
                                x_aggregate(q + 1)
                            if i == 3:
                                x_dev(q + 1)
                            if i == 5:
                                x_rstd(q + 1)
                    link(last)
                    v.memset(scratch[:], 0.0)
                    last = v.bn_aggr(ymv[:, q * GQ + GQ - 1, :], yparts[:, GQ - 1, :])
                last.then_inc(S["y_parts"], 1)
                dve.wait_ge(S["y_mean"], n + 1)
                v.tensor_copy(mean1[:], ps[:, 0, 0:G])
                link(v.tensor_tensor(dev[:], ymv[:, :, 0], ps[:, 0, 0:G], ALU.subtract))
                link(v.tensor_tensor(dev[:], dev[:], dev[:], ALU.mult))
                v.tensor_tensor(dev[:], dev[:], ymv[:, :, 1], ALU.add).then_inc(S["y_dev"], 1)
                dve.wait_ge(S["y_sd"], n + 1)
                link(newton(rstd1[:], tiny[:], ps[:, 1, 0:G], G))
                member = tab("member", HALF).rearrange("p (s g) -> p s g", s=2)
                for j, src in enumerate((rstd1, mean1)):
                    last = v.tensor_tensor(prod[:, j], member,
                                           src[0:HALF].rearrange("p (s g) -> p s g", s=1).broadcast_to([HALF, 2, G]), ALU.mult)
                link(last)
                link(v.tensor_reduce(col1[:].rearrange("p a b -> p (a b)"), prod[:].rearrange("p a b g -> p (a b) g"), AX.X, ALU.add))
                for half in range(2):
                    v.tensor_scalar(w1s[:, half, :], w1t_sb[:, half, :], col1[:, 0, half:half + 1], None, ALU.mult)
                    last = v.tensor_scalar(mrep[:, half, :], tab("average", HALF), col1[:, 1, half:half + 1], 128.0,
                                           ALU.mult, ALU.mult)
                last.then_inc(S["mix_w"], 1)

                def turned_b(b):
                    dve.wait_ge(S["y_turned"], n * 32 + b + 1)
                    if b >= 4:
                        dve.wait_ge(S["mixed"], n * 32 + b - 3)
                    v.tensor_copy(work_r[0:HALF, b % 4, 512:1024], ps[0:HALF, 3 + 2 * (b % 3), :]).then_inc(S["turned_b"], 1)

                turned_b(0)
                dve.wait_ge(S["mix_bias"], n + 1)
                v.tensor_tensor(bias_1[:], bias_0[:], ps[:, 1, 64:64 + C1], ALU.subtract)
                turned_b(1)
                link(v.tensor_scalar(tiny[:], mean0[:], wraw0[:, 9:10], None, ALU.add))
                link(v.tensor_tensor(const_o[0:T].rearrange("p (g c) w -> p g (c w)", g=G),
                                     tiny[0:T].rearrange("p (g c) -> p g c", c=1).broadcast_to([T, G, 2 * CG]),
                                     tab("lane12", T).rearrange("p (g c) -> p g c", g=1).broadcast_to([T, G, 2 * CG]),
                                     ALU.mult))
                v.scalar_tensor_tensor(blk_o[0:T], blk_o[0:T], tab("keep", T), const_o[0:T], ALU.mult, ALU.add)\
                    .then_inc(S["mix_ready"], 1)
                dve.wait_ge(S["mix_ready"], n + 1)

                def mix_out(u):
                    dve.wait_ge(S["mixed"], n * 32 + 2 * u + 2)
                    v.tensor_tensor(mix[:, 8 * u:8 * u + 8, 0:C1],
                                    ps[:, u % 2, 0:8 * C1].rearrange("p (w o) -> p w o", w=8),
                                    bias_1[:].rearrange("p (w o) -> p w o", w=1).broadcast_to([128, 8, C1]), ALU.add)\
                        .then_inc(S["mix_out"], 1)

                for b in range(2, 32):
                    turned_b(b)
                    if b >= 5 and b % 2:
                        mix_out((b - 5) // 2)
                mix_out(14)
                mix_out(15)

                def plane_2_out(u):
                    dve.wait_ge(S["plane_2"], n * 2 * PAIRS + u + 1)
                    v.tensor_copy(re_im(0)[:, :, 2 * u:2 * u + 2, :],
                                  ps[:, 2 + u % 4, :].rearrange("p (c r w) -> p r c w", c=2, r=2))\
                        .then_inc(S["plane_2_out_r"], 1)

                def inverse(j):
                    dve.wait_ge(S["magnitude"], n * NL + j + 1)
                    v.scalar_tensor_tensor(lot(j, 3), lot(j, 2), 1e-30, lot(j, 3), ALU.max, ALU.add).then_inc(S["inverse"], 1)
                    dve.wait_ge(S["inverse"], (n * NL + j) * 2 + 1)
                    v.reciprocal(lot(j, 3), lot(j, 3)).then_inc(S["inverse"], 1)

                def signs(j):
                    dve.wait_ge(S["tangent"], n * NL + j + 1)
                    v.tensor_scalar(lot(j, 1), lot(j, 1), 0.0, 0.5, ALU.is_ge, ALU.subtract)
                    v.tensor_scalar(lot(j, 0), lot(j, 0), 0.0, None, ALU.is_lt).then_inc(S["sign"], 1)

                def phase(j):
                    dve.wait_ge(S["sign"], n * NL + j + 1)
                    dve.wait_ge(S["arctan"], n * NL + j + 1)
                    v.scalar_tensor_tensor(lot(j, 3), lot(j, 0), 0.5, lot(j, 3), ALU.subtract, ALU.mult).then_inc(S["fold"], 1)
                    dve.wait_ge(S["fold"], n * NL + j + 1)
                    dve.wait_ge(S["corner"], n * NL + j + 1)
                    v.scalar_tensor_tensor(lot(j, 3), lot(j, 1), -math.pi / 2, lot(j, 3), ALU.mult, ALU.add).then_inc(S["phase"], 1)

                def box_out(t):
                    m = min(4, NBOX - 4 * t)
                    dve.wait_ge(S["box_turned"], n * 4 + t + 1)
                    src = ps[:, t % 2, 0:m * 128].rearrange("p (j h) -> p j h", j=m)[:, :, LO:LO + BOX]
                    dst = boxed[:, 4 * t:4 * t + m, LO + 1:LO + BOX + 1]
                    a, b = (1 if t == 0 else 0), (m - 1 if t == 3 else m)
                    if t == 0:
                        v.tensor_scalar(dst[:, 0, :], src[:, 0, :], tab("edge")[:, 0:1], None, ALU.mult)
                    if t == 3:
                        v.tensor_scalar(dst[:, m - 1, :], src[:, m - 1, :], tab("edge")[:, 1:2], None, ALU.mult)
                    v.tensor_copy(dst[:, a:b, :], src[:, a:b, :]).then_inc(S["box_turned_out"], 1)

                def mixed_out(j):
                    k, a, blocks = UNITS[j]
                    first, end = (KW - 1, KW) if blocks == 1 else (a, a + WB * blocks)
                    dve.wait_ge(S["mag_mixed"], n * NU + j + 1)
                    for m, bias in enumerate((bias_c, bias_q) if k else (bias_f, bias_p)):
                        inner = (max(first, LO), min(end, LO + BOX)) if k == 0 and m == 0 else (end, end)
                        for lo, hi, inside in ((first, inner[0], False), (*inner, True), (max(inner[1], first), end, False)):
                            if lo >= hi or (not inside and (lo, hi) == (end, end)):
                                continue
                            o = buf(k, 2 + m)[:, C0 * lo:C0 * hi].rearrange("p (w o) -> p w o", o=C0)
                            i = ps[:, 6 + m, C0 * (lo - a):C0 * (hi - a)].rearrange("p (w o) -> p w o", o=C0)
                            z = (bias_in if inside else bias)[:].rearrange("p (w o) -> p w o", w=1).broadcast_to([128, hi - lo, C0])
                            if inside:
                                last = v.scalar_tensor_tensor(o, i, tab("rows")[:, 1:2], z, ALU.mult, ALU.add)
                            else:
                                last = v.tensor_tensor(o, i, z, ALU.add)
                    last.then_inc(S["mixed_out"], 1)

                def whole(j):
                    dve.wait_ge(S["mixed_out"], n * NU + (j + 1 if j < 5 else NU))
                    v.tensor_scalar(sl(j, 0), sl(j, 3), ROUND, ROUND, ALU.add, ALU.subtract).then_inc(S["whole"], 1)

                def conv_out(t):
                    dve.wait_ge(S["box_mixed"], n * 3 + t + 1)
                    c = C0 * (LO + 30 * t)
                    o = work_r[:, 2, c:c + 480]
                    v.scalar_tensor_tensor(o, ps[:, (2 + t) % 4, 0:480], tab("rows")[:, 0:1], o, ALU.mult, ALU.add)\
                        .then_inc(S["box_mixed_out"], 1)

                def z_re(j):
                    dve.wait_ge(S["sine"], (n * NS + j) * 2 + 2)
                    if j < 4:
                        dve.wait_ge(S["box_mixed_out"], n * 3 + min(j + 1, 3))
                    v.tensor_tensor(sl(j, 0), sl(j, 2), sl(j, 3), ALU.mult).then_inc(S["z_re"], 1)

                for u in range(4):
                    plane_2_out(u)
                inverse(0)
                plane_2_out(4)
                plane_2_out(5)
                inverse(1)
                signs(0)
                plane_2_out(6)
                plane_2_out(7)
                inverse(2)
                signs(1)
                inverse(3)
                phase(0)
                signs(2)
                phase(1)
                signs(3)
                phase(2)
                phase(3)
                inverse(4)
                inverse(5)
                box_out(0)
                mixed_out(0)
                box_out(1)
                box_out(2)
                whole(0)
                mixed_out(1)
                box_out(3)
                whole(1)
                signs(4)
                conv_out(0)
                mixed_out(2)
                whole(2)
                conv_out(1)
                mixed_out(3)
                whole(3)
                z_re(0)
                z_re(1)
                conv_out(2)
                z_re(2)
                z_re(3)
                signs(5)
                phase(4)
                phase(5)
                mixed_out(4)
                whole(4)
                mixed_out(5)
                mixed_out(6)
                whole(5)
                z_re(4)
                z_re(5)
                for u in range(PAIRS, 2 * PAIRS):
                    p = u - PAIRS
                    dve.wait_ge(S["back_2"], n * 2 * PAIRS + u + 1)
                    v.tensor_copy(mix[:, :, 2 * C0 + 2 * p:2 * C0 + 2 * p + 2].rearrange("p w c -> p c w"),
                                  ps[:, 2 + u % 2, 0:256].rearrange("p (c w) -> p c w", c=2)).then_inc(S["back_copied"], 1)
                for t in range(1, 16, 2):
                    dve.wait_ge(S["t_turned"], n * 16 + t + 1)
                    v.tensor_copy(work_r[0:T, t // 4, 512 * (t % 4):512 * (t % 4) + 512], ps[0:T, t % 4, :])\
                        .then_inc(S["t_turned_dve"], 1)
                for u, (c, m, w, i) in enumerate(FINAL_UNITS):
                    dve.wait_ge(S["final"], n * NF + u + 1)
                    y = image[:, c:c + m, 2 * w * i:2 * w * (i + 1)].rearrange("p c (b w) -> p b c w", b=2)
                    o = ps[:, FINAL_BANK[u % 4]:FINAL_BANK[u % 4] + 2, 0:w * m].rearrange("p b (c w) -> p b c w", w=w)
                    v.tensor_tensor(y, y, o, ALU.add).then_inc(S["final_out"], 1)
                    if more and NF - GQ - 2 <= u < NF - 2:
                        x_stats(n + 1, 0, u - (NF - GQ - 2))
                    if more and u == NF - 2:
                        x_aggregate(0)

            with dve.Fori(0, N - 1) as n:
                one_image(n, True)
            assert linked[0] - SETUP_LINKS == LINKS, linked[0] - SETUP_LINKS
            one_image(N - 1, False)


def kernel(x, L0_conv_w, L0_conv_b, L1_conv_conv1_w, L1_conv_mag_s_w, L1_conv_mag_s_b, L1_conv_mag_f_w,
           L1_conv_mag_f_b, L1_conv_mag_w, L1_conv_mag_b, L1_conv_pha_w, L1_conv_pha_b, L1_conv_conv_0_w,
           L1_conv_conv_0_b, L1_conv_conv_1_w, L1_conv_conv_1_b, L1_conv_conv2_w):
    import concourse.bacc as bacc
    from concourse.bass_utils import run_bass_kernel_spmd

    tables, once, at = constant_tables()
    row = lambda a: np.ascontiguousarray(a).reshape(1, -1)
    col = lambda a: np.ascontiguousarray(a).reshape(-1, 1)
    turned = lambda a: np.ascontiguousarray(np.asarray(a).T)
    arrays = dict(
        x=np.ascontiguousarray(x), tables=tables, once=once, l0_w=row(L0_conv_w), l0_b=row(L0_conv_b),
        w1=np.ascontiguousarray(L1_conv_conv1_w), w1_t=turned(L1_conv_conv1_w),
        ws=np.ascontiguousarray(L1_conv_mag_s_w).reshape(C0, C0 * 9), ws_b=col(L1_conv_mag_s_b),
        wf_in=np.ascontiguousarray(L1_conv_mag_f_w), wf_b=col(L1_conv_mag_f_b),
        ww_t=turned(L1_conv_mag_w), ww_b=row(L1_conv_mag_b), wp_t=turned(L1_conv_pha_w), wp_b=row(L1_conv_pha_b),
        w0_t=turned(L1_conv_conv_0_w), w0_b=row(L1_conv_conv_0_b),
        wc_t=turned(L1_conv_conv_1_w), wc_b=row(L1_conv_conv_1_b), w2_t=turned(L1_conv_conv2_w))
    nc = bacc.Bacc("TRN2", target_bir_lowering=False, num_devices=1)
    nc.disable_value_cache = True
    aps = {k: nc.dram_tensor(k, a.shape, mybir.dt.float32, kind="ExternalInput").ap() for k, a in arrays.items()}
    out = nc.dram_tensor("out", arrays["x"].shape, mybir.dt.float32, kind="ExternalOutput").ap()
    build(nc, at=at, out=out, **aps)
    return run_bass_kernel_spmd(nc, [arrays], core_ids=[0]).results[0]["out"]
```
